# Optimizing a Trainium2 kernel written in Bass

```python
import numpy as np
import jax
import jax.numpy as jnp

def _softmax(x, axis=-1):
    return jax.nn.softmax(x, axis=axis)

def _gelu(x):
    return jax.nn.gelu(x, approximate=True)

def _silu(x):
    return jax.nn.silu(x)

def _sigmoid(x):
    return jax.nn.sigmoid(x)

def _layernorm(x, axis=-1, eps=1e-05):
    m = jnp.mean(x, axis=axis, keepdims=True)
    v = jnp.var(x, axis=axis, keepdims=True)
    return (x - m) / jnp.sqrt(v + eps)

def _scatter_add(tgt, idx, src, axis=0):
    return tgt.at[idx].add(src)

def _segment_sum(src, seg, n):
    return jax.ops.segment_sum(src, seg, n)
kernel_name = 'mk_gnn_preln_d2_gnn_r64_f4a013'

def setup_inputs(seed: int=0):
    np.random.seed(seed)
    _w = jnp.asarray

    def _rec_inputs():
        import jax
        import jax.numpy as jnp
        _gk = jax.random.key(seed)
        x = -0.0007083 + 1.001 * jax.random.normal(jax.random.fold_in(_gk, 1), (100000, 48), jnp.float32)
        src = jax.random.randint(jax.random.fold_in(_gk, 2), (50000,), 0, 100000, jnp.int32)
        dst = jnp.minimum((100000 * jax.random.uniform(jax.random.fold_in(_gk, 3), (50000,)) ** 2.0).astype(jnp.int32), 99999)
        _o = jnp.argsort(dst, stable=True)
        src = src[_o]
        dst = dst[_o]
        edge_attr_40 = jax.random.uniform(jax.random.fold_in(_gk, 13), (50000, 40), jnp.float32, 0.0, 1)
        edge_weight = jax.random.uniform(jax.random.fold_in(_gk, 15), (50000,), jnp.float32, 0.0, 6.99999)
        node_type_119 = jax.random.randint(jax.random.fold_in(_gk, 16), (100000,), 0, 119, jnp.int32)
        node_vec = jax.random.uniform(jax.random.fold_in(_gk, 17), (100000,), jnp.float32, 0.0, 1.49999)
        return (x, src, dst, edge_attr_40, edge_weight, node_type_119, node_vec)
    x, src, dst, edge_attr_40, edge_weight, node_type_119, node_vec = _rec_inputs()

    def _L0_gnn_setup():
        import jax, jax.numpy as jnp
        import numpy as np
        CUTOFF = 6.0
        LN_EPS = 1e-05
        key = jax.random.key(seed)
        ks = jax.random.split(key, 16)
        N, E, H, R, NEL, G = (50000, 12500, 48, 40, 119, 32)
        inp = {'h': jax.random.normal(ks[0], (N, H), jnp.float32), 'edge_index': jax.random.randint(ks[1], (2, E), 0, N, jnp.int64), 'edge_attr': jax.random.uniform(ks[2], (E, R), jnp.float32), 'distances': jax.random.uniform(ks[3], (E,), jnp.float32) * 7.0, 'atom_z': jax.random.randint(ks[4], (N,), 0, NEL, jnp.int64), 'node_mult': jax.random.uniform(ks[5], (N,), jnp.float32) + 0.5, 'batch': jnp.zeros((N,), jnp.int64), 'W1': jax.random.normal(ks[6], (H, R), jnp.float32) / np.sqrt(R), 'b1': jax.random.normal(ks[7], (H,), jnp.float32) * 0.01, 'W2': jax.random.normal(ks[8], (H, H), jnp.float32) / np.sqrt(H), 'b2': jax.random.normal(ks[9], (H,), jnp.float32) * 0.01, 'emb': jax.random.normal(ks[10], (NEL, G), jnp.float32) * 0.01, 'adaptW': jax.random.normal(ks[11], (G, G), jnp.float32) * 0.01, 'gamma': jnp.ones((H,), jnp.float32), 'beta': jnp.zeros((H,), jnp.float32)}
        return inp
    _L0_gnn_all = _L0_gnn_setup()
    _L0_gnn_in = {k: v for k, v in _L0_gnn_all.items() if k in ('W1', 'b1', 'W2', 'b2', 'emb', 'adaptW', 'gamma', 'beta')}
    del _L0_gnn_all

    def _L1_gnn_setup():
        import jax, jax.numpy as jnp
        import numpy as np
        N_NODES = 100000
        N_EDGES = 25000
        D_FEAT = 48
        N_LAYERS = 2
        key = jax.random.key(seed)
        k1, k2, k3 = jax.random.split(key, 3)
        row = jax.random.randint(k1, (N_EDGES,), 0, N_NODES, dtype=jnp.int32)
        col = jax.random.randint(k2, (N_EDGES,), 0, N_NODES, dtype=jnp.int32)
        x = jax.random.normal(k3, (N_NODES, D_FEAT), dtype=jnp.float32)
        return {'row': row, 'col': col, 'x': x}
    _L1_gnn_all = _L1_gnn_setup()
    _L1_gnn_in = {k: v for k, v in _L1_gnn_all.items() if k in ()}
    del _L1_gnn_all
    return {'x': x, 'src': src, 'dst': dst, 'edge_attr_40': edge_attr_40, 'edge_weight': edge_weight, 'node_type_119': node_type_119, 'node_vec': node_vec, 'L0_gnn_W1': _L0_gnn_in['W1'], 'L0_gnn_b1': _L0_gnn_in['b1'], 'L0_gnn_W2': _L0_gnn_in['W2'], 'L0_gnn_b2': _L0_gnn_in['b2'], 'L0_gnn_emb': _L0_gnn_in['emb'], 'L0_gnn_adaptW': _L0_gnn_in['adaptW'], 'L0_gnn_gamma': _L0_gnn_in['gamma'], 'L0_gnn_beta': _L0_gnn_in['beta']}

def reference(x, src, dst, edge_attr_40, edge_weight, node_type_119, node_vec, L0_gnn_W1, L0_gnn_b1, L0_gnn_W2, L0_gnn_b2, L0_gnn_emb, L0_gnn_adaptW, L0_gnn_gamma, L0_gnn_beta):
    import jax
    import jax.numpy as jnp

    def _L0_gnn_ref(h, edge_index, edge_attr, distances, atom_z, node_mult, batch, W1, b1, W2, b2, emb, adaptW, gamma, beta):
        import jax, jax.numpy as jnp
        import numpy as np
        CUTOFF = 6.0
        LN_EPS = 1e-05
        src, dst = (edge_index[0], edge_index[1])
        N = h.shape[0]
        gate = jax.nn.silu(edge_attr @ W1.T + b1) @ W2.T + b2
        ei = emb[atom_z[src]]
        ej = emb[atom_z[dst]]
        adapt_logit = jnp.sum(ei * (ej @ adaptW.T), axis=-1, keepdims=True)
        gate = gate + adapt_logit
        cw = jnp.where(distances < CUTOFF, 0.5 * (jnp.cos(jnp.pi * distances / CUTOFF) + 1.0), 0.0)
        mj = node_mult[dst]
        msg = gate * h[dst] * (cw * mj)[:, None]
        agg = jax.ops.segment_sum(msg, src, num_segments=N)
        tot = jax.ops.segment_sum(mj, src, num_segments=N)
        agg = agg / jnp.clip(tot, 1e-08, None)[:, None]
        x = h + agg
        mu = jnp.mean(x, axis=-1, keepdims=True)
        var = jnp.mean(jnp.square(x - mu), axis=-1, keepdims=True)
        return (x - mu) / jnp.sqrt(var + LN_EPS) * gamma + beta

    def _L1_gnn_ref(row, col, x):
        import jax, jax.numpy as jnp
        import numpy as np
        N_NODES = 100000
        N_EDGES = 25000
        D_FEAT = 48
        N_LAYERS = 2
        n = x.shape[0]
        loop = jnp.arange(n, dtype=row.dtype)
        r = jnp.concatenate([row, loop])
        c = jnp.concatenate([col, loop])
        deg = jax.ops.segment_sum(jnp.ones(r.shape, dtype=x.dtype), r, num_segments=n)
        dinv = jnp.where(deg > 0, jax.lax.rsqrt(deg), 0.0)
        w = dinv[r] * dinv[c]
        for _ in range(N_LAYERS):
            x = jax.ops.segment_sum(w[:, None] * x[c], r, num_segments=n)
        return x
    edge_index = jnp.stack([src, dst])
    batch0 = jnp.zeros((100000,), jnp.int32)
    h = jnp.maximum(_layernorm(x, axis=-1), 0.0)
    x = x + _L0_gnn_ref(h, edge_index, edge_attr_40, edge_weight, node_type_119, node_vec, batch0, L0_gnn_W1, L0_gnn_b1, L0_gnn_W2, L0_gnn_b2, L0_gnn_emb, L0_gnn_adaptW, L0_gnn_gamma, L0_gnn_beta)
    h = jnp.maximum(_layernorm(x, axis=-1), 0.0)
    x = x + _L1_gnn_ref(src, dst, h)
    return x

_drawn_inputs = setup_inputs


def setup_inputs(seed=0):
    import zlib

    import numpy as np

    out = dict(_drawn_inputs(seed))
    spreads = {'L0_gnn_gamma': (1.0, 0.2), 'L0_gnn_beta': (0.0, 0.1)}
    factors = {'node_vec': 51.359,
     'L0_gnn_b1': 52.207,
     'L0_gnn_b2': 34.778,
     'L0_gnn_emb': 64.0,
     'L0_gnn_adaptW': 64.0}
    for name, (base, spread) in spreads.items():
        noise = np.random.default_rng([zlib.crc32(name.encode()), seed]).standard_normal(out[name].shape)
        drawn = base * np.exp(spread * noise) if base else spread * noise
        out[name] = jnp.asarray(drawn.astype(out[name].dtype))
    for name, factor in factors.items():
        out[name] = (out[name] * factor).astype(out[name].dtype)
    return out
```

```python
from contextlib import ExitStack

import concourse.bass as bass
from concourse import mybir

F32 = mybir.dt.float32
I32 = mybir.dt.int32
BF16 = mybir.dt.bfloat16
ALU = mybir.AluOpType
ACT = mybir.ActivationFunctionType
AX = mybir.AxisListType.X

P = 128
N = 100000
H = 48
R = 40
NZ = 119
G = 32
J = 783
NP = P * J
NPACK = 3
JZ = J // NPACK
U = 7
C = 392
NB = C // U
E = C * P
GROUPS = (range(0, 4), range(4, 7))
MW = H + 2
JT = 27
NT = J // JT
CUTOFF = 6.0
EPS = 1e-5
PI = 3.141592653589793
ROUND = 12582912.0
assert NP >= N and JZ * NPACK == J and NB % 2 == 0 and JT * NT == J and NT % 2 == 1
CSRC, CDST, ESRC, SPARE, CUT = range(5)
NF = 5


def in_pairs(eng, n, step):
    for r in range(3):
        step(0, r)
    pairs = (n - 1) // 2
    with eng.Fori(1, pairs) as i:
        step(i, 1)
        step(i, 2)
    if n - 1 > 2 * pairs:
        step(pairs, 1)


SETUP = 30
CHAIN = 21
CHAIN_D = (19, 3, 3)
STORES = (3, 2, 1)


def landed(eng, i, r, s_sca):
    chunks = U * (r - 1)
    for q in range(2):
        eng.wait_ge(s_sca[q], (i * U + (chunks + 1 - q) // 2) * 16)


def half(i, r):
    return i + r // 2


def build(nc, xm, src_col, dst_col, w_col, src_row, dst_row, attrT, types, w1T, b1, w2T, b2, embT,
          adaptT, gamma, beta, out):
    ctx = ExitStack()
    with ctx:
        def sb(name, shape, dt=F32):
            return ctx.enter_context(nc.sbuf_tensor(name, shape, dt))

        def ps(name, shape, dt=F32):
            return ctx.enter_context(nc.psum_tensor(name, shape, dt))

        def sem(name):
            return ctx.enter_context(nc.semaphore(name))

        def dram(name, rows, width):
            return nc.dram_tensor(name, [rows, width], F32, kind="Internal").ap()

        sums = [[dram(f"sums{l}_{q}", NP + P, MW if l == 0 else H) for q in range(2)] for l in range(3)]
        gtab = [dram(f"gtab{l}", NP, H) for l in range(2)]
        x1tab = dram("x1tab", NP, H)

        zero = sb("zero", [P, 56 * MW])
        ident = sb("ident", [P, P], BF16)
        identf = sb("identf", [P, P])
        before = sb("before", [P, P])
        iota_f = sb("iota_f", [P, JZ])
        iota_b = sb("iota_b", [P, NZ], BF16)
        part = sb("part", [P, 1])
        ncentre = sb("ncentre", [P, 1])
        epsc = sb("epsc", [P, 1])
        w1T_s = sb("w1T_s", [R, H])
        b1_s = sb("b1_s", [H, 1])
        w2_s = sb("w2_s", [H + 1, H])
        embT_s = sb("embT_s", [G, NZ])
        adT_s = sb("adT_s", [G, G])
        u_s = sb("u_s", [G, NZ])
        tt_s = sb("tt_s", [NZ, NZ])
        gam = sb("gam", [P, H])
        bet = sb("bet", [P, H])
        ztab_i = sb("ztab_i", [P, J], I32)
        ztab = sb("ztab", [P, JZ])
        dsti = sb("dsti", [P, C + 2 * U], I32)
        srci = sb("srci", [P, C], I32)
        srcf = sb("srcf", [P, C])
        wcol = sb("wcol", [P, C])
        t0 = sb("t0", [P, 2, C])
        t1 = sb("t1", [P, 2, C])
        t2 = sb("t2", [P, 2, C])
        ec = sb("ec", [P, C, NF])
        shi = sb("shi", [P, C, 2], I32)
        sidx = sb("sidx", [P, C], I32)
        srow = sb("srow", [P, 2, U * P], I32)
        drow = sb("drow", [P, 2, U * P], I32)
        att = sb("att", [R, 2, U * P])
        dist = sb("dist", [P, 2, U * P])
        mask = sb("mask", [P, 2, U * P])
        bc = sb("bc", [P, U, NF])
        bsh = sb("bsh", [P, U, 2], I32)
        gidx = sb("gidx", [P, 2, U], I32)
        scidx = sb("scidx", [P, 2, U], I32)
        xg = sb("xg", [P, 2, U, H + 1])
        zq = sb("zq", [P, U, 2])
        zi = sb("zi", [P, U, 2], I32)
        zi2 = sb("zi2", [P, U, 2], I32)
        zi3 = sb("zi3", [P, U, 2], I32)
        zf = sb("zf", [P, U, 2])
        oh = sb("oh", [P, U, NZ], BF16)
        ohT = sb("ohT", [NZ, U * P])
        hT = sb("hT", [H + 1, U * P])
        junk = sb("junk", [P, 2, JZ])
        junkd = sb("junkd", [P, 2, P])
        junka = sb("junka", [P, U, NZ])
        adap = sb("adap", [P, U])
        same = sb("same", [P, 2, U, P])
        dup = sb("dup", [P, U])
        dupn = sb("dupn", [P, U])
        sx = sb("sx", [P, U])
        xc = sb("xc", [P, U, H])
        xcn = sb("xcn", [P, U, H])
        sq = sb("sq", [P, U, H])
        ss = sb("ss", [P, U])
        sd = sb("sd", [P, U])
        rs = sb("rs", [P, U])
        cw = sb("cw", [P, U])
        gg = sb("gg", [P, U, H])
        gw = sb("gw", [P, U, H])
        gx = sb("gx", [P, 2, U, H])
        msg = sb("msg", [P, U, MW])
        sm = sb("sm", [P, 2, U, MW])
        dinv = sb("dinv", [P, J])
        dx = sb("dx", [P, 2, JT, H])
        da = sb("da", [P, 2, JT, MW])
        dh = sb("dh", [P, JT, H])
        dc = sb("dc", [P, JT, H])
        dq = sb("dq", [P, JT, H])
        dy = sb("dy", [P, 2, JT, H])
        do = sb("do", [P, 2, JT, H])
        r0 = sb("r0", [P, JT])
        r1 = sb("r1", [P, JT])
        r2 = sb("r2", [P, JT])
        r3 = sb("r3", [P, JT])
        rd = sb("rd", [P, JT])

        p_z = ps("p_z", [P, 2, 512])
        p_h = ps("p_h", [H, 512])
        p_g = ps("p_g", [P, U, H])
        p_t = ps("p_t", [NZ, U * P], BF16)
        p_v = ps("p_v", [P, 8, P])
        p_s = ps("p_s", [P, U, MW])

        s_const = sem("s_const")
        s_cols = sem("s_cols")
        s_iota = sem("s_iota")
        s_spare = sem("s_spare")
        s_zero = sem("s_zero")
        s_zeroed = [sem(f"s_zeroed{l}") for l in range(3)]
        s_u = sem("s_u")
        s_uc = sem("s_uc")
        s_sin = sem("s_sin")
        s_arg = sem("s_arg")
        s_set = sem("s_set")
        s_nop = {e: sem(f"s_nop_{e}") for e in ("pool", "act", "dve", "pe", "sp")}
        s_row = [sem(f"s_row{q}") for q in range(2)]
        s_att = [sem(f"s_att{q}") for q in range(2)]
        s_dist = sem("s_dist")
        s_mask = sem("s_mask")
        s_zp = sem("s_zp")
        s_zr = sem("s_zr")
        s_same = sem("s_same")
        s_chain = sem("s_chain")
        s_oh = sem("s_oh")
        s_tr = sem("s_tr")
        s_trc = sem("s_trc")
        s_tv = sem("s_tv")
        s_ad = sem("s_ad")
        s_hid = sem("s_hid")
        s_silu = sem("s_silu")
        s_gate = sem("s_gate")
        s_gru = sem("s_gru")
        s_gidx = sem("s_gidx")
        s_gat = [sem(f"s_gat{q}") for q in range(2)]
        s_xc = sem("s_xc")
        s_sq = sem("s_sq")
        s_ss = sem("s_ss")
        s_sd = sem("s_sd")
        s_msg = sem("s_msg")
        s_sidx = sem("s_sidx")
        s_sum = sem("s_sum")
        s_smc = sem("s_smc")
        s_sca = [sem(f"s_sca{q}") for q in range(2)]
        L = []
        for l in (1, 2):
            L.append(dict(
                row=[sem(f"t{l}_row{q}") for q in range(2)], same=sem(f"t{l}_same"), gidx=sem(f"t{l}_gidx"),
                gat=[sem(f"t{l}_gat{q}") for q in range(2)], sum=sem(f"t{l}_sum"), smc=sem(f"t{l}_smc"),
                sidx=sem(f"t{l}_sidx"), stage=sem(f"t{l}_stage"), sca=[sem(f"t{l}_sca{q}") for q in range(2)]))
        D = []
        for l in range(3):
            D.append(dict(
                x=[sem(f"d{l}_x{q}") for q in range(2)], a=[sem(f"d{l}_a{q}") for q in range(2)],
                acc=[sem(f"d{l}_acc{q}") for q in range(2)], chain=sem(f"d{l}_chain"), used=sem(f"d{l}_used"),
                sq=sem(f"d{l}_sq"), sqd=sem(f"d{l}_sqd"), act=sem(f"d{l}_act"),
                made=sem(f"d{l}_made"), out=[sem(f"d{l}_out{q}") for q in range(2)]))

        block = ctx.enter_context(nc.Block())

        def hold(eng, name, s, v):
            eng.wait_ge(s, v)
            eng.nop().then_inc(s_nop[name], 1)

        def rows_of(table, t):
            return table[0:NP, :].rearrange("(p j) f -> p (j f)", p=P)[
                :, bass.ds(t * (JT * table.shape[1]), JT * table.shape[1])]

        BODY = P * (J + 1)
        assert BODY == NP + P and (J + 1) % 56 == 0

        def zero_table(eng, table, done):
            view = table.rearrange("(p j) f -> p (j f)", p=P)
            w = 56 * table.shape[1]
            for c in range((J + 1) // 56):
                eng.dma_start(view[:, c * w:(c + 1) * w], zero[:, 0:w]).then_inc(done, 16)

        ZD = 16 * ((J + 1) // 56)
        assert (J + 1) == 28 * ((NB - 2) // 2 + 1)

        def zero_slice(eng, l, i):
            w = 28 * H
            eng.dma_start(sums[l][1].rearrange("(p j) f -> p (j f)", p=P)[:, bass.ds(i * w, w)],
                          zero[:, 0:w]).then_inc(s_zeroed[l], 16)

        def tile_of(buf, q, w):
            return buf[:, q, :, :].rearrange("p j f -> p (j f)")[:, 0:JT * w].rearrange("p (j f) -> p j f", f=w)

        @block.sync
        def _(sp):
            sp.dma_start(dsti[:], dst_col).then_inc(s_cols, 16)
            sp.dma_start(srci[:], src_col).then_inc(s_cols, 16)
            sp.dma_start(wcol[:], w_col).then_inc(s_cols, 16)
            sp.dma_start(ztab_i[:], types).then_inc(s_cols, 16)
            sp.wait_ge(s_zero, 1)
            for q in range(2):
                zero_table(sp, sums[0][q], s_zeroed[0])
            for l in (1, 2):
                sp.dma_start(sums[l][0][NP:NP + P, :], zero[:, 0:H]).then_inc(s_zeroed[l], 16)

            def load_batch(i, r):
                q = r % 2
                b = i * 2 + r
                cols = bass.ds(b * (U * P), U * P)
                sp.dma_start(srow[:, q, :], src_row[0:1, cols].to_broadcast([P, U * P])).then_inc(s_row[q], 16)
                sp.dma_start(drow[:, q, :], dst_row[0:1, cols].to_broadcast([P, U * P])).then_inc(s_row[q], 16)
                sp.dma_start(att[:, q, :], attrT[:, cols]).then_inc(s_att[q], 16)

            load_batch(0, 0)
            load_batch(0, 1)

            def prefetch(i, r):
                b = i * 2 + r
                hold(sp, "sp", s_same, b * U)
                hold(sp, "sp", s_hid, b * 2)
                load_batch(i, r + 1)

            with sp.Fori(0, (NB - 2) // 2) as i:
                prefetch(i, 1)
                prefetch(i, 2)
                zero_slice(sp, 1, i)
            zero_slice(sp, 1, (NB - 2) // 2)

            for l in range(3):
                d = D[l]
                if l > 0:
                    t = L[l - 1]

                    def load_rows(i, r, t=t):
                        q = r % 2
                        cols = bass.ds((i * 2 + r) * (U * P), U * P)
                        sp.dma_start(srow[:, q, :], src_row[0:1, cols].to_broadcast([P, U * P])).then_inc(t["row"][q], 16)

                    if l == 1:
                        sp.wait_ge(s_same, NB * U)
                    else:
                        sp.wait_ge(L[0]["same"], NB)
                    load_rows(0, 0)
                    load_rows(0, 1)
                    with sp.Fori(0, (NB - 2) // 2) as i:
                        for r in (1, 2):
                            hold(sp, "sp", t["same"], i * 2 + r)
                            load_rows(i, r + 1)
                        if l == 1:
                            zero_slice(sp, 2, i)
                    if l == 1:
                        zero_slice(sp, 2, (NB - 2) // 2)
                sca = s_sca if l == 0 else L[l - 1]["sca"]
                for q in range(2):
                    sp.wait_ge(sca[q], 16 * C // 2)

                def load_tile(i, r, l=l, d=d):
                    q = r % 2
                    t = i * 2 + r
                    if l == 0:
                        sp.dma_start(dx[:, q, :, :].rearrange("p j f -> p (j f)"),
                                     xm[0:NP, 0:H].rearrange("(p j) f -> p j f", p=P)[:, bass.ds(t * JT, JT), :]
                                     ).then_inc(d["x"][q], 16)
                    if l == 2:
                        sp.dma_start(dx[:, q, :, :].rearrange("p j f -> p (j f)"), rows_of(x1tab, t)).then_inc(d["x"][q], 16)
                    w = MW if l == 0 else H
                    sp.dma_start(da[:, q, :, :].rearrange("p j f -> p (j f)")[:, 0:JT * w],
                                 rows_of(sums[l][0], t)).then_inc(d["a"][q], 16)

                def store_tile(i, r, l=l, d=d):
                    q = r % 2
                    t = i * 2 + r
                    hold(sp, "sp", d["made"], t + 1)
                    y = dy[:, q, :, :].rearrange("p j f -> p (j f)")
                    o = do[:, q, :, :].rearrange("p j f -> p (j f)")
                    if l == 0:
                        sp.dma_start(rows_of(x1tab, t), y).then_inc(d["out"][q], 16)
                    if l < 2:
                        sp.dma_start(rows_of(gtab[l], t), o).then_inc(d["out"][q], 16)
                        sp.dma_start(rows_of(sums[l + 1][0], t), o).then_inc(d["out"][q], 16)
                    else:
                        sp.dma_start(rows_of(out, t), o).then_inc(d["out"][q], 16)

                load_tile(0, 0)
                load_tile(0, 1)

                def turn(i, r, l=l, d=d):
                    store_tile(i, r)
                    hold(sp, "sp", d["used"], i * 2 + r + 1)
                    load_tile(i, r + 2)

                turn(0, 0)
                with sp.Fori(0, (NT - 3) // 2) as i:
                    turn(i, 1)
                    turn(i, 2)
                store_tile((NT - 3) // 2, 1)
                store_tile((NT - 3) // 2, 2)
                for q in range(2):
                    sp.wait_ge(d["out"][q], 16 * STORES[l] * (NT // 2 + (q == 0)))

        @block.gpsimd
        def _(pool):
            pool.iota(iota_f[:], [[1, JZ]], base=0, channel_multiplier=0,
                      allow_small_or_imprecise_dtypes=True).then_inc(s_iota, 1)
            pool.iota(iota_b[:], [[1, NZ]], base=0, channel_multiplier=0,
                      allow_small_or_imprecise_dtypes=True).then_inc(s_iota, 1)
            pool.iota(part[:], [[0, 1]], base=0, channel_multiplier=1,
                      allow_small_or_imprecise_dtypes=True).then_inc(s_iota, 1)
            pool.iota(ncentre[:], [[0, 1]], base=-(J - 1) // 2, channel_multiplier=-J,
                      allow_small_or_imprecise_dtypes=True).then_inc(s_iota, 1)
            pool.memset(before[:], 1.0).then_inc(s_iota, 1)
            pool.memset(ident[:], 0.0).then_inc(s_iota, 1)
            pool.wait_ge(s_iota, 6)
            pool.affine_select(out=before[:], in_=before[:], compare_op=ALU.is_gt, fill=0.0, base=0,
                               pattern=[[-1, P]], channel_multiplier=1).then_inc(s_iota, 1)
            pool.affine_select(out=ident[:], in_=ident[:], compare_op=ALU.not_equal, fill=1.0, base=0,
                               pattern=[[-1, P]], channel_multiplier=1).then_inc(s_iota, 1)

            def edge_pass(table, width, dst_tables, s_gi, s_g, rows, s_si, s_sm, s_sc, rows_free, zeroed):
                def gather(q, k):
                    pool.indirect_dma_start(rows[:, q, k, :], None, table,
                                            bass.IndirectOffsetOnAxis(gidx[:, q, k:k + 1], 0)).then_inc(s_g[q], 16)

                def scatter(i, r, k):
                    c = U * r + k
                    q = c % 2
                    before_it = i * U + c // 2
                    if isinstance(before_it, int):
                        if before_it > 0:
                            pool.wait_ge(s_sc[q], 16 * before_it)
                    else:
                        hold(pool, "pool", s_sc[q], before_it * 16)
                    pool.indirect_dma_start(dst_tables[q], bass.IndirectOffsetOnAxis(scidx[:, r % 2, k:k + 1], 0),
                                            sm[:, r % 2, k, 0:width], None, compute_op=ALU.add).then_inc(s_sc[q], 16)

                def ready(i, r):
                    b = i * 2 + r
                    hold(pool, "pool", s_gi, b + 1)
                    s_free, per = rows_free
                    if isinstance(b, int):
                        if b >= 2:
                            hold(pool, "pool", s_free, (b - 1) * per)
                    else:
                        hold(pool, "pool", s_free, (b - 1) * per)

                def sums_ready(i, r):
                    b = i * 2 + r
                    hold(pool, "pool", s_sm, b + 1)
                    hold(pool, "pool", s_si, b + 1)

                def step(i, r):
                    ready(i, r)
                    for k in range(U):
                        gather(r % 2, k)
                        if k == 0:
                            sums_ready(i, r - 2)
                        scatter(i, r - 2, k)

                for r in range(2):
                    ready(0, r)
                    for k in range(U):
                        gather(r, k)
                for s, v in zeroed:
                    pool.wait_ge(s, v)
                step(0, 2)
                step(0, 3)
                with pool.Fori(1, (NB - 2) // 2) as i:
                    step(i, 2)
                    step(i, 3)
                for r in range(2):
                    sums_ready((NB - 2) // 2, r)
                    for k in range(U):
                        scatter((NB - 2) // 2, r, k)

            def accumulate(l):
                d = D[l]
                w = MW if l == 0 else H

                def step(i, r):
                    q = r % 2
                    hold(pool, "pool", d["a"][q], (half(i, r) + 1) * 16)
                    pool.dma_start(da[:, q, :, :].rearrange("p j f -> p (j f)")[:, 0:JT * w],
                                   rows_of(sums[l][1], i * 2 + r), accum_op=ALU.add).then_inc(d["acc"][q], 16)
                in_pairs(pool, NT, step)

            edge_pass(xm, MW, sums[0], s_gidx, s_gat, xg, s_sidx, s_smc, s_sca, (s_msg, 1), [(s_zeroed[0], 2 * ZD)])
            for q in range(2):
                pool.wait_ge(s_sca[q], 16 * C // 2)
            accumulate(0)
            for l in (1, 2):
                t = L[l - 1]
                for q in range(2):
                    pool.wait_ge(D[l - 1]["out"][q], 16 * STORES[l - 1] * (NT // 2 + (q == 0)))
                edge_pass(gtab[l - 1], H, sums[l], t["gidx"], t["gat"], gx, t["sidx"], t["smc"], t["sca"],
                          (t["sum"], 1), [(s_zeroed[l], 16 * (NB // 2) + 16)])
                for q in range(2):
                    pool.wait_ge(t["sca"][q], 16 * C // 2)
                accumulate(l)

        @block.scalar
        def _(act):
            act.dma_start(w1T_s[:], w1T).then_inc(s_const, 16)
            act.dma_start(b1_s[:], b1).then_inc(s_const, 16)
            act.dma_start(w2_s[0:H, :], w2T).then_inc(s_const, 16)
            act.dma_start(w2_s[H:H + 1, :], b2).then_inc(s_const, 16)
            act.dma_start(embT_s[:], embT).then_inc(s_const, 16)
            act.dma_start(adT_s[:], adaptT).then_inc(s_const, 16)
            act.dma_start(gam[:], gamma.to_broadcast([P, H])).then_inc(s_const, 16)
            act.dma_start(bet[:], beta.to_broadcast([P, H])).then_inc(s_const, 16)
            act.wait_ge(s_iota, 8)
            act.activation(identf[:], ident[:], ACT.Copy).then_inc(s_uc, 1)
            act.wait_ge(s_u, 1)
            act.activation(u_s[:], p_v[0:G, 0, 0:NZ], ACT.Copy).then_inc(s_uc, 1)
            act.wait_ge(s_u, 2)
            act.activation(tt_s[:], p_v[0:NZ, 1, 0:NZ], ACT.Copy).then_inc(s_uc, 1)
            act.wait_ge(s_arg, 1)
            act.activation(t1[:, 1, :], t1[:, 0, :], ACT.Sin, scale=PI / (2 * CUTOFF)).then_inc(s_sin, 1)

            def distances(i, r):
                q = r % 2
                b = i * 2 + r
                act.wait_ge(s_row[q], (half(i, r) + 1) * 32)
                if not isinstance(b, int) or b > 0:
                    act.wait_ge(s_mask, b * 2)
                for w, rows in enumerate((srow, drow)):
                    act.activation(dist[:, w, :], rows[:, q, :], ACT.Abs, bias=ncentre[:, 0:1]).then_inc(s_dist, 1)

            def step(i, r):
                b = i * 2 + r
                first = isinstance(b, int) and b == 0
                for m in range(2):
                    act.wait_ge(s_hid, b * 2 + m + 1)
                    if not first:
                        act.wait_ge(s_gate, b)
                    act.activation(hT[0:H, m * (U * P // 2):(m + 1) * (U * P // 2)], p_h[:, 0:U * P // 2],
                                   ACT.Silu, bias=b1_s[:, 0:1]).then_inc(s_silu, 1)
                act.wait_ge(s_tr, b + 1)
                if not first:
                    act.wait_ge(s_tv, b * 2)
                act.activation(ohT[:], p_t[:], ACT.Copy).then_inc(s_trc, 1)
                act.wait_ge(s_xc, b + 1)
                act.activation(sq[:], xc[:], ACT.Square).then_inc(s_sq, 1)
                act.wait_ge(s_ss, b + 1)
                act.activation(sd[:], ss[:], ACT.Sqrt, scale=1.0 / H, bias=epsc[:, 0:1]).then_inc(s_sd, 1)
                if not (isinstance(i, int) and b == NB - 1):
                    distances(i, r + 1)
                copy_sums(i, r, s_sum, s_smc, s_sca, MW)

            def copy_sums(i, r, s_sum, s_smc, s_sca, w):
                b = i * 2 + r
                act.wait_ge(s_sum, b + 1)
                if not isinstance(b, int) or b >= 2:
                    landed(act, i, r, s_sca)
                act.activation(sm[:, r % 2, :, 0:w], p_s[:, :, 0:w], ACT.Copy).then_inc(s_smc, 1)

            act.wait_ge(s_iota, 8)
            act.wait_ge(s_const, 8 * 16)
            act.wait_ge(s_set, SETUP)
            distances(0, 0)
            in_pairs(act, NB, step)

            def squares(l):
                d = D[l]

                def step(i, r):
                    t = i * 2 + r
                    n = 0
                    for part_ in range(3):
                        act.wait_ge(d["sq"], t * 7 + n + 1)
                        act.activation(dq[:], dc[:], ACT.Square).then_inc(d["act"], 1)
                        n += 1
                        act.wait_ge(d["sq"], t * 7 + n + 1)
                        act.activation(rd[:], r1[:], ACT.Sqrt, scale=1.0 / H, bias=epsc[:, 0:1]).then_inc(d["act"], 1)
                        n += 1
                    act.wait_ge(d["sq"], t * 7 + n + 1)
                    act.activation(rd[:], da[:, r % 2, :, H + 1], ACT.Sqrt, bias=1.0).then_inc(d["act"], 1)
                in_pairs(act, NT, step)

            squares(0)
            for l in (1, 2):
                t = L[l - 1]
                in_pairs(act, NB, lambda i, r: copy_sums(i, r, t["sum"], t["smc"], t["sca"], H))

        @block.tensor
        def _(pe):
            pe.wait_ge(s_const, 8 * 16)
            pe.matmul(p_v[0:G, 0, 0:NZ], adT_s[:], embT_s[:], start=True, stop=True).then_inc(s_u, 1)
            pe.wait_ge(s_uc, 2)
            pe.matmul(p_v[0:NZ, 1, 0:NZ], u_s[:], embT_s[:], start=True, stop=True).then_inc(s_u, 1)
            pe.wait_ge(s_uc, 3)
            pe.wait_ge(s_set, SETUP)

            def step(i, r):
                q = r % 2
                b = i * 2 + r
                first = isinstance(b, int) and b == 0
                hold(pe, "pe", s_att[q], (half(i, r) + 1) * 16)
                hw = U * P // 2
                for m in range(2):
                    if not (first and m == 0):
                        hold(pe, "pe", s_silu, b * 2 + m)
                    pe.matmul(p_h[:, 0:hw], w1T_s[:], att[:, q, m * hw:(m + 1) * hw], start=True, stop=True).then_inc(s_hid, 1)
                pe.wait_ge(s_mask, b * 2 + 2)
                for k in range(U):
                    for w in range(2):
                        if not (first and k == 0):
                            pe.wait_ge(s_zr, b * (2 * U) + 2 * k + w - 1)
                        pe.matmul(p_z[:, w, 0:JZ], mask[:, w, k * P:(k + 1) * P], ztab[:], start=True, stop=True).then_inc(s_zp, 1)
                pe.wait_ge(s_silu, b * 2 + 2)
                if not first:
                    pe.wait_ge(s_gru, b)
                for k in range(U):
                    last = pe.matmul(p_g[:, k, :], hT[:, k * P:(k + 1) * P], w2_s[:], start=True, stop=True)
                last.then_inc(s_gate, 1)
                pe.wait_ge(s_oh, (b + 1) * U)
                if not first:
                    pe.wait_ge(s_trc, b)
                for k in range(U):
                    last = pe.transpose(p_t[:, k * P:(k + 1) * P], oh[:, k, :], ident[:])
                last.then_inc(s_tr, 1)
                pe.wait_ge(s_trc, b + 1)
                for g, ks in enumerate(GROUPS):
                    if not first:
                        pe.wait_ge(s_ad, (b - 1) * U + ks[-1] + 1)
                    for k in ks:
                        last = pe.matmul(p_v[:, k, 0:NZ], ohT[:, k * P:(k + 1) * P], tt_s[:], start=True, stop=True)
                    last.then_inc(s_tv, 1)
                sum_batch(i, r, msg, MW, s_msg, s_sum, s_smc)

            def sum_batch(i, r, rows, w, s_rows, s_sum, s_smc):
                b = i * 2 + r
                first = isinstance(b, int) and b == 0
                pe.wait_ge(s_rows, b + 1)
                if not first:
                    pe.wait_ge(s_smc, b)
                for k in range(U):
                    last = pe.matmul(p_s[:, k, 0:w], same[:, r % 2, k, :], rows[:, k, :], start=True, stop=True)
                last.then_inc(s_sum, 1)

            in_pairs(pe, NB, step)

            for l in (1, 2):
                t = L[l - 1]

                def step(i, r):
                    q = r % 2
                    pe.wait_ge(t["gat"][q], (half(i, r) + 1) * (16 * U))
                    sum_batch(i, r, gx[:, q, :, :], H, t["same"], t["sum"], t["smc"])
                in_pairs(pe, NB, step)

        @block.vector
        def _(dve):
            dve.memset(zero[:], 0.0).then_inc(s_zero, 1)
            n = [0]

            def do_(ins):
                n[0] += 1
                ins.then_inc(s_set, 1)
                dve.wait_ge(s_set, n[0])

            do_(dve.memset(hT[:], 1.0))
            do_(dve.memset(msg[:], 1.0))
            do_(dve.memset(epsc[:], EPS))
            dve.wait_ge(s_iota, 8)
            dve.wait_ge(s_cols, 64)
            do_(dve.tensor_scalar(t0[:, 0, :], wcol[:], 1.0 / (2 * CUTOFF), ROUND, ALU.mult, ALU.add))
            do_(dve.tensor_scalar(t0[:, 1, :], t0[:, 0, :], -ROUND, None, ALU.add))
            n[0] += 1
            dve.scalar_tensor_tensor(t1[:, 0, :], t0[:, 1, :], -2.0 * CUTOFF, wcol[:], ALU.mult, ALU.add).then_inc(s_arg, 1)
            n[0] -= 1
            do_(dve.scalar_tensor_tensor(junk[:, 0, :], ztab_i[:, JZ:2 * JZ], 128.0, ztab_i[:, 0:JZ], ALU.mult, ALU.add))
            do_(dve.scalar_tensor_tensor(ztab[:], ztab_i[:, 2 * JZ:3 * JZ], 16384.0, junk[:, 0, :], ALU.mult, ALU.add))
            do_(dve.tensor_copy(srcf[:], srci[:]))
            do_(dve.tensor_copy(ec[:, :, ESRC], srcf[:]))
            do_(dve.tensor_scalar(rd[:, 0:1], part[:], float(NP), None, ALU.add))
            do_(dve.tensor_scalar(ec[:, :, SPARE], srcf[:], -1.0, rd[:, 0:1], ALU.mult, ALU.add))
            dve.wait_ge(s_sin, 1)
            do_(dve.tensor_tensor(t0[:, 0, :], t1[:, 1, :], t1[:, 1, :], ALU.mult))
            do_(dve.tensor_scalar(t0[:, 1, :], t0[:, 0, :], -1.0, 1.0, ALU.mult, ALU.add))
            do_(dve.scalar_tensor_tensor(ec[:, :, CUT], wcol[:], CUTOFF, t0[:, 1, :], ALU.is_lt, ALU.mult))
            for w, idx in enumerate((srci[:], dsti[:, 0:C])):
                do_(dve.tensor_scalar(t0[:, 0, :], idx, 0.5, 1.0 / J, ALU.add, ALU.mult))
                do_(dve.tensor_scalar(t0[:, 1, :], t0[:, 0, :], -0.5, ROUND, ALU.add, ALU.add))
                do_(dve.tensor_scalar(t0[:, 0, :], t0[:, 1, :], -ROUND, None, ALU.add))
                do_(dve.scalar_tensor_tensor(t1[:, 0, :], t0[:, 0, :], -float(J), idx, ALU.mult, ALU.add))
                do_(dve.tensor_scalar(t2[:, 0, :], t1[:, 0, :], float(JZ), None, ALU.is_ge))
                do_(dve.scalar_tensor_tensor(t2[:, 1, :], t1[:, 0, :], float(2 * JZ), t2[:, 0, :], ALU.is_ge, ALU.add))
                do_(dve.scalar_tensor_tensor(ec[:, :, CSRC + w], t2[:, 1, :], -float(JZ), t1[:, 0, :], ALU.mult, ALU.add))
                do_(dve.tensor_scalar(shi[:, :, w], t2[:, 1, :], 7.0, None, ALU.mult))
            for r in range(2):
                dve.tensor_copy(gidx[:, r, :], dsti[:, r * U:(r + 1) * U]).then_inc(s_gidx, 1)
            assert n[0] == SETUP, n[0]

            count = [0]

            def step(i, r):
                q = r % 2
                b = i * 2 + r
                first = isinstance(b, int) and b == 0
                count[0] = 0

                def chain(ins):
                    count[0] += 1
                    ins.then_inc(s_chain, 1)
                    return count[0]

                def after(v):
                    dve.wait_ge(s_chain, b * CHAIN + v)

                cols = bass.ds(b * U, U)
                chain(dve.tensor_copy(bc[:], ec[:, cols, :]))
                v_bc = chain(dve.tensor_copy(bsh[:], shi[:, cols, :]))
                for w in range(2):
                    dve.wait_ge(s_dist, b * 2 + w + 1)
                    if not first:
                        dve.wait_ge(s_zp, b * (2 * U))
                    dve.tensor_scalar(mask[:, w, :], dist[:, w, :], J / 2, None, ALU.is_lt).then_inc(s_mask, 1)
                after(v_bc)
                dve.wait_ge(s_row[q], (half(i, r) + 1) * 32)
                if not isinstance(b, int) or b >= 2:
                    dve.wait_ge(s_sum, b - 1)
                for k in range(U):
                    for w in range(2):
                        dve.wait_ge(s_zp, b * (2 * U) + 2 * k + w + 1)
                        dve.scalar_tensor_tensor(junk[:, w, :], iota_f[:], bc[:, k, w:w + 1], p_z[:, w, 0:JZ], ALU.is_equal,
                                                 ALU.mult, accum_out=zq[:, k, w:w + 1]).then_inc(s_zr, 1)
                    v_dup = chain(dve.scalar_tensor_tensor(junkd[:, k % 2, :], srow[:, q, k * P:(k + 1) * P],
                                                           bc[:, k, ESRC:ESRC + 1], before[:], ALU.is_equal, ALU.mult,
                                                           accum_out=dup[:, k:k + 1]))
                    dve.tensor_scalar(same[:, q, k, :], srow[:, q, k * P:(k + 1) * P], bc[:, k, ESRC:ESRC + 1], None,
                                      ALU.is_equal).then_inc(s_same, 1)
                dve.wait_ge(s_zr, (b + 1) * (2 * U))
                after(chain(dve.tensor_copy(zi[:], zq[:])))
                after(chain(dve.tensor_tensor(zi2[:], zi[:], bsh[:], ALU.logical_shift_right)))
                after(chain(dve.tensor_scalar(zi3[:], zi2[:], 127, None, ALU.bitwise_and)))
                after(chain(dve.tensor_copy(zf[:], zi3[:])))
                if not first:
                    dve.wait_ge(s_tr, b)
                for k in range(U):
                    dve.tensor_scalar(oh[:, k, :], iota_b[:], zf[:, k, 1:2], None, ALU.is_equal).then_inc(s_oh, 1)
                dve.wait_ge(s_gat[q], (half(i, r) + 1) * (16 * U))
                v = chain(dve.reduce_sum(sx[:], xg[:, q, :, 0:H], axis=AX))
                after(v)
                if not first:
                    dve.wait_ge(s_sq, b)
                dve.scalar_tensor_tensor(xc[:], sx[:].unsqueeze(2).to_broadcast([P, U, H]), -1.0 / H, xg[:, q, :, 0:H],
                                         ALU.mult, ALU.add).then_inc(s_xc, 1)
                v = chain(dve.scalar_tensor_tensor(dupn[:], dup[:], 1.0, bc[:, :, SPARE], ALU.min, ALU.mult))
                after(v)
                chain(dve.tensor_tensor(sidx[:, cols], dupn[:], bc[:, :, ESRC], ALU.add))
                if not isinstance(b, int) or b >= 2:
                    landed(dve, i, r, s_sca)
                dve.tensor_tensor(scidx[:, q, :], dupn[:], bc[:, :, ESRC], ALU.add).then_inc(s_sidx, 1)
                if not (isinstance(b, int) and b == NB - 1):
                    dve.tensor_copy(gidx[:, q, :], dsti[:, bass.ds(b * U + 2 * U, U)]).then_inc(s_gidx, 1)
                dve.wait_ge(s_sq, b + 1)
                dve.reduce_sum(ss[:], sq[:], axis=AX).then_inc(s_ss, 1)
                chain(dve.tensor_tensor(cw[:], bc[:, :, CUT], xg[:, q, :, H], ALU.mult))
                for k in range(U):
                    if k in (GROUPS[0][0], GROUPS[1][0]):
                        dve.wait_ge(s_tv, b * 2 + (1 if k == 0 else 2))
                    dve.scalar_tensor_tensor(junka[:, k, :], iota_f[:, 0:NZ], zf[:, k, 0:1], p_v[:, k, 0:NZ],
                                             ALU.is_equal, ALU.mult, accum_out=adap[:, k:k + 1]).then_inc(s_ad, 1)
                dve.wait_ge(s_sd, b + 1)
                after(chain(dve.reciprocal(rs[:], sd[:])))
                v_x = chain(dve.tensor_tensor(xcn[:], xc[:], rs[:].unsqueeze(2).to_broadcast([P, U, H]), ALU.mult))
                dve.wait_ge(s_gate, b + 1)
                dve.wait_ge(s_ad, (b + 1) * U)
                dve.tensor_tensor(gg[:], p_g[:], adap[:].unsqueeze(2).to_broadcast([P, U, H]), ALU.add).then_inc(s_gru, 1)
                dve.wait_ge(s_gru, b + 1)
                v_w = chain(dve.tensor_tensor(gw[:], gg[:], cw[:].unsqueeze(2).to_broadcast([P, U, H]), ALU.mult))
                if not first:
                    dve.wait_ge(s_sum, b)
                chain(dve.tensor_copy(msg[:, :, H], xg[:, q, :, H]))
                after(v_w)
                dve.scalar_tensor_tensor(msg[:, :, 0:H], xcn[:], 0.0, gw[:], ALU.max, ALU.mult).then_inc(s_msg, 1)
                assert count[0] == CHAIN, count[0]

            in_pairs(dve, NB, step)

            def wide(v):
                return v.unsqueeze(2).to_broadcast([P, JT, H])

            def dense(l):
                d = D[l]

                def step(i, r):
                    q = r % 2
                    t = i * 2 + r
                    count[0] = 0
                    asked = [0]

                    def chain(ins):
                        count[0] += 1
                        ins.then_inc(d["chain"], 1)
                        dve.wait_ge(d["chain"], t * CHAIN_D[l] + count[0])

                    def ask(ins):
                        asked[0] += 1
                        ins.then_inc(d["sq"], 1)
                        dve.wait_ge(d["act"], t * 7 + asked[0])

                    def deviation(rows):
                        chain(dve.reduce_sum(r0[:], rows, axis=AX))
                        ask(dve.scalar_tensor_tensor(dc[:], wide(r0[:]), -1.0 / H, rows, ALU.mult, ALU.add))
                        ask(dve.reduce_sum(r1[:], dq[:], axis=AX))
                        chain(dve.reciprocal(r2[:], rd[:]))

                    cols = bass.ds(t * JT, JT)
                    w = MW if l == 0 else H
                    a = tile_of(da, q, w)
                    if l != 1:
                        dve.wait_ge(d["x"][q], (half(i, r) + 1) * 16)
                    x = dx[:, q, :, :]
                    if l == 0:
                        deviation(x)
                        chain(dve.scalar_tensor_tensor(dh[:], dc[:], 0.0, wide(r2[:]), ALU.max, ALU.mult))
                        dve.wait_ge(d["acc"][q], (half(i, r) + 1) * 16)
                        chain(dve.tensor_scalar(r3[:], a[:, :, H], 1e-8, None, ALU.max))
                        chain(dve.reciprocal(r0[:], r3[:]))
                        chain(dve.tensor_tensor(dc[:], a[:, :, 0:H], wide(r0[:]), ALU.mult))
                        chain(dve.tensor_tensor(dh[:], dh[:], dc[:], ALU.add))
                        deviation(dh[:])
                        chain(dve.tensor_tensor(dh[:], dc[:], wide(r2[:]), ALU.mult))
                        chain(dve.tensor_tensor(dc[:], dh[:], gam[:].unsqueeze(1).to_broadcast([P, JT, H]), ALU.mult))
                        chain(dve.tensor_tensor(dh[:], dc[:], bet[:].unsqueeze(1).to_broadcast([P, JT, H]), ALU.add))
                        if not isinstance(t, int) or t >= 2:
                            dve.wait_ge(d["out"][q], half(i, r) * (16 * STORES[l]))
                        chain(dve.tensor_tensor(dy[:, q, :, :], dh[:], x, ALU.add))
                        deviation(dy[:, q, :, :])
                        ask(dve.tensor_copy(r3[:], r2[:]))
                        chain(dve.reciprocal(r0[:], rd[:]))
                        chain(dve.tensor_copy(dinv[:, cols], r0[:]))
                        chain(dve.tensor_tensor(r1[:], r3[:], r0[:], ALU.mult))
                        chain(dve.scalar_tensor_tensor(do[:, q, :, :], dc[:], 0.0, wide(r1[:]), ALU.max, ALU.mult))
                    else:
                        dve.wait_ge(d["acc"][q], (half(i, r) + 1) * 16)
                        if not isinstance(t, int) or t >= 2:
                            dve.wait_ge(d["out"][q], half(i, r) * (16 * STORES[l]))
                        chain(dve.tensor_scalar(r0[:], dinv[:, cols], 1.0, None, ALU.mult))
                        if l == 1:
                            chain(dve.tensor_tensor(r1[:], r0[:], r0[:], ALU.mult))
                            chain(dve.tensor_tensor(do[:, q, :, :], a, wide(r1[:]), ALU.mult))
                        else:
                            chain(dve.tensor_tensor(dh[:], a, wide(r0[:]), ALU.mult))
                            chain(dve.tensor_tensor(do[:, q, :, :], dh[:], x, ALU.add))
                    dve.nop().then_inc(d["used"], 1)
                    dve.nop().then_inc(d["made"], 1)
                    assert count[0] == CHAIN_D[l], count[0]
                in_pairs(dve, NT, step)

            dense(0)

            for l in (1, 2):
                t = L[l - 1]
                for r in range(2):
                    dve.tensor_copy(gidx[:, r, :], dsti[:, r * U:(r + 1) * U]).then_inc(t["gidx"], 1)

                def step(i, r):
                    q = r % 2
                    b = i * 2 + r
                    cols = bass.ds(b * U, U)
                    if not isinstance(b, int) or b > 0:
                        hold(dve, "dve", t["same"], b)
                    dve.tensor_copy(bc[:, :, 0], srcf[:, cols]).then_inc(t["stage"], 1)
                    dve.wait_ge(t["stage"], b + 1)
                    dve.wait_ge(t["row"][q], (half(i, r) + 1) * 16)
                    if not isinstance(b, int) or b >= 2:
                        dve.wait_ge(t["sum"], b - 1)
                    for k in range(U):
                        last = dve.tensor_scalar(same[:, q, k, :], srow[:, q, k * P:(k + 1) * P], bc[:, k, 0:1], None, ALU.is_equal)
                    last.then_inc(t["same"], 1)
                    if not isinstance(b, int) or b >= 2:
                        landed(dve, i, r, t["sca"])
                        hold(dve, "dve", t["sidx"], b)
                    dve.tensor_copy(scidx[:, q, :], sidx[:, cols]).then_inc(t["sidx"], 1)
                    if not (isinstance(b, int) and b == NB - 1):
                        hold(dve, "dve", t["gat"][q], (half(i, r) + 1) * (16 * U))
                        dve.tensor_copy(gidx[:, q, :], dsti[:, bass.ds(b * U + 2 * U, U)]).then_inc(t["gidx"], 1)
                in_pairs(dve, NB, step)
                dense(l)


def kernel(x, src, dst, edge_attr_40, edge_weight, node_type_119, node_vec, L0_gnn_W1, L0_gnn_b1, L0_gnn_W2,
           L0_gnn_b2, L0_gnn_emb, L0_gnn_adaptW, L0_gnn_gamma, L0_gnn_beta):
    import numpy as np
    import concourse.bacc as bacc
    from concourse.bass_utils import run_bass_kernel_spmd

    def padded(a, n, fill=0):
        a = np.asarray(a)
        out = np.zeros((n,) + a.shape[1:], a.dtype)
        out[:a.shape[0]] = a
        if not isinstance(fill, int):
            out[a.shape[0]:] = fill
        return out

    spare = (NP + np.arange(E) % P).astype(np.int32)[np.asarray(src).shape[0]:]
    srcp = padded(src, E, spare)
    dstp = padded(dst, E)

    def by_chunk(a):
        return np.ascontiguousarray(a.reshape(C, P).T)

    arrays = {
        "xm": padded(np.concatenate([np.asarray(x), np.asarray(node_vec)[:, None]], axis=1), NP),
        "src_col": by_chunk(srcp),
        "dst_col": np.concatenate([by_chunk(dstp), np.zeros((P, 2 * U), dstp.dtype)], axis=1),
        "w_col": by_chunk(padded(edge_weight, E)),
        "src_row": srcp[None, :],
        "dst_row": dstp[None, :],
        "attrT": np.ascontiguousarray(padded(edge_attr_40, E).T),
        "types": padded(node_type_119, NP).reshape(P, J),
        "w1T": np.ascontiguousarray(np.asarray(L0_gnn_W1).T),
        "b1": np.asarray(L0_gnn_b1)[:, None],
        "w2T": np.ascontiguousarray(np.asarray(L0_gnn_W2).T),
        "b2": np.asarray(L0_gnn_b2)[None, :],
        "embT": np.ascontiguousarray(np.asarray(L0_gnn_emb).T),
        "adaptT": np.ascontiguousarray(np.asarray(L0_gnn_adaptW).T),
        "gamma": np.asarray(L0_gnn_gamma)[None, :],
        "beta": np.asarray(L0_gnn_beta)[None, :],
    }
    nc = bacc.Bacc("TRN2", target_bir_lowering=False, num_devices=1)
    args = [nc.dram_tensor(k, a.shape, mybir.dt.from_np(a.dtype), kind="ExternalInput").ap() for k, a in arrays.items()]
    args.append(nc.dram_tensor("result", (NP, H), F32, kind="ExternalOutput").ap())
    build(nc, *args)
    got = run_bass_kernel_spmd(nc, [arrays], core_ids=[0])
    return got.results[0]["result"][:N]
```

```python
from contextlib import ExitStack

import concourse.bass as bass
from concourse import mybir

F32 = mybir.dt.float32
I32 = mybir.dt.int32
BF16 = mybir.dt.bfloat16
ALU = mybir.AluOpType
ACT = mybir.ActivationFunctionType
AX = mybir.AxisListType.X

P = 128
N = 100000
H = 48
R = 40
NZ = 119
G = 32
J = 784
NP = P * J
NPACK = 3
JZ = 261
JN = JZ * NPACK
U = 7
C = 392
NB = C // U
E = C * P
GROUPS = (range(0, 4), range(4, 7))
MW = H + 2
JT = 28
NT = J // JT
CUTOFF = 6.0
EPS = 1e-5
PI = 3.141592653589793
ROUND = 12582912.0
assert NP >= N and P * JN >= N and NB % 2 == 0 and JT * NT == J and NT % 2 == 0
CSRC, CDST, ESRC, SPARE, BASE, CUT = range(6)
NF = 6


def in_pairs(eng, n, step):
    for r in range(3):
        step(0, r)
    pairs = (n - 1) // 2
    with eng.Fori(1, pairs) as i:
        step(i, 1)
        step(i, 2)
    if n - 1 > 2 * pairs:
        step(pairs, 1)


SETUP = 33
CHAIN = 13
CHAIN_D = {"a": 6, "b": 4, "c": 5, 1: 2, 2: 2}
PAIRS = NT // 2
STORES = (3, 2, 1)


def landed(eng, i, r, s_sca):
    chunks = U * (r - 1)
    for q in range(2):
        eng.wait_ge(s_sca[q], (i * U + (chunks + 1 - q) // 2) * 16)


def half(i, r):
    return i + r // 2


def build(nc, xm, src_col, dst_col, w_col, src_row, dst_row, attrT, types, w1T, b1, w2T, b2, embT,
          adaptT, gamma, beta, out):
    ctx = ExitStack()
    with ctx:
        def sb(name, shape, dt=F32):
            return ctx.enter_context(nc.sbuf_tensor(name, shape, dt))

        def ps(name, shape, dt=F32):
            return ctx.enter_context(nc.psum_tensor(name, shape, dt))

        def sem(name):
            return ctx.enter_context(nc.semaphore(name))

        def dram(name, rows, width):
            return nc.dram_tensor(name, [rows, width], F32, kind="Internal").ap()

        sums = [[dram(f"sums{l}_{q}", NP + P, MW if l == 0 else H) for q in range(2)] for l in range(3)]
        gtab = [dram(f"gtab{l}", NP, H) for l in range(2)]
        x1tab = dram("x1tab", NP, H)

        zero = sb("zero", [P, 56 * MW])
        ident = sb("ident", [P, P], BF16)
        identf = sb("identf", [P, P])
        upto = sb("upto", [P, P])
        iota_f = sb("iota_f", [P, JZ])
        iota_b = sb("iota_b", [P, NZ], BF16)
        part = sb("part", [P, 1])
        ncentre = sb("ncentre", [P, 1])
        epsc = sb("epsc", [P, 1])
        w1T_s = sb("w1T_s", [R, H])
        b1_s = sb("b1_s", [H, 1])
        w2_s = sb("w2_s", [H + 1, H])
        embT_s = sb("embT_s", [G, NZ])
        adT_s = sb("adT_s", [G, G])
        u_s = sb("u_s", [G, NZ])
        tt_s = sb("tt_s", [NZ, NZ])
        gam = sb("gam", [P, H])
        bet = sb("bet", [P, H])
        ztab_i = sb("ztab_i", [P, JN], I32)
        ztab = sb("ztab", [P, NPACK, JZ], BF16)
        dsti = sb("dsti", [P, C + 2 * U], I32)
        srci = sb("srci", [P, C], I32)
        srcf = sb("srcf", [P, C])
        wcol = sb("wcol", [P, C])
        st = sb("st", [P, 2, JT, H])
        flat = st[:].rearrange("p q j f -> p (q j f)")
        t0, t1, t2 = (flat[:, m * 2 * C:(m + 1) * 2 * C].rearrange("p (a c) -> p a c", a=2) for m in range(3))
        ec = sb("ec", [P, C, NF])
        shi = sb("shi", [P, C, 2], I32)
        sidx = sb("sidx", [P, C], I32)
        srow = sb("srow", [P, 2, U * P], I32)
        drow = sb("drow", [P, 2, U * P], I32)
        att = sb("att", [R, 2, U * P])
        npp = sb("npp", [P, 1])
        xb = sb("xb", [P, 2, JT, H])
        dist = xb[:].rearrange("p q j f -> p (q j f)")[:, 0:2 * U * P].rearrange("p (a e) -> p a e", a=2)
        mask = sb("mask", [P, 2, U * P], BF16)
        bc = sb("bc", [P, U, NF])
        bsh = sb("bsh", [P, U, 2], I32)
        gidx = sb("gidx", [P, 2, U], I32)
        scidx = sb("scidx", [P, 2, U], I32)
        xg = sb("xg", [P, 2, U, H + 1])
        zq = sb("zq", [P, U, 2])
        zi = sb("zi", [P, U, 2], I32)
        zi2 = sb("zi2", [P, U, 2], I32)
        zi3 = sb("zi3", [P, U, 2], I32)
        zf = sb("zf", [P, U, 2])
        oh = sb("oh", [P, U, NZ], BF16)
        ohT = sb("ohT", [NZ, U * P])
        hT = sb("hT", [H + 1, U * P])
        junk = sb("junk", [P, 2, JZ])
        junkd = sb("junkd", [P, 2, P])
        junka = sb("junka", [P, U, NZ])
        adap = sb("adap", [P, U])
        same = sb("same", [P, 2, U, P])
        dup = sb("dup", [P, U])
        dupn = sb("dupn", [P, U])
        sx = sb("sx", [P, U])
        nm = sb("nm", [P, U])
        hn = sb("hn", [P, U, H])
        sq = sb("sq", [P, U, H])
        nmr = sb("nmr", [P, U])
        ss = sb("ss", [P, U])
        sd = sb("sd", [P, U])
        rs = sb("rs", [P, U])
        cw = sb("cw", [P, U])
        gg = sb("gg", [P, U, H])
        gw = sb("gw", [P, U, H])
        gx = sb("gx", [P, 2, U, H])
        msg = sb("msg", [P, U, MW])
        sm = sb("sm", [P, 2, U, MW])
        dinv = sb("dinv", [P, J])
        dx = sb("dx", [P, 2, JT, H + 1])
        da = sb("da", [P, 2, JT, MW])
        dh = sb("dh", [P, 2, JT, H])
        dc = sb("dc", [P, 2, JT, H])
        dq = sb("dq", [P, 2, JT, H])
        dy = sb("dy", [P, 2, JT, H])
        do = sb("do", [P, 2, JT, H])
        rsum = sb("rsum", [P, 2, JT])
        rsq = sb("rsq", [P, 2, JT])
        rroot = sb("rroot", [P, 2, JT])
        rinv = {m: sb(f"rinv_{m}", [P, 2, JT]) for m in "abc"}
        rtot = sb("rtot", [P, 2, JT])
        itot = sb("itot", [P, 2, JT])
        rdeg = sb("rdeg", [P, 2, JT])
        fac = sb("fac", [P, 2 * JT])
        fac2 = sb("fac2", [P, 2 * JT])
        ones = sb("ones", [P, 2 * JT])
        assert 6 * C <= 2 * JT * H and 2 * U * P <= 2 * JT * H

        p_z = ps("p_z", [P, 2, 512])
        p_h = ps("p_h", [H, 512])
        p_g = ps("p_g", [P, U, H])
        p_t = ps("p_t", [NZ, U * P], BF16)
        p_v = ps("p_v", [P, 8, P])
        p_s = ps("p_s", [P, U, MW])

        s_const = sem("s_const")
        s_cols = sem("s_cols")
        s_iota = sem("s_iota")
        s_spare = sem("s_spare")
        s_zero = sem("s_zero")
        s_zeroed = [sem(f"s_zeroed{l}") for l in range(3)]
        s_u = sem("s_u")
        s_uc = sem("s_uc")
        s_sin = sem("s_sin")
        s_arg = sem("s_arg")
        s_set = sem("s_set")
        s_nop = {e: sem(f"s_nop_{e}") for e in ("pool", "act", "dve", "pe", "sp")}
        s_row = [sem(f"s_row{q}") for q in range(2)]
        s_att = [sem(f"s_att{q}") for q in range(2)]
        s_dist = sem("s_dist")
        s_mask = sem("s_mask")
        s_zp = sem("s_zp")
        s_zr = sem("s_zr")
        s_same = sem("s_same")
        s_chain = sem("s_chain")
        s_oh = sem("s_oh")
        s_tr = sem("s_tr")
        s_trc = sem("s_trc")
        s_tv = sem("s_tv")
        s_ad = sem("s_ad")
        s_hid = sem("s_hid")
        s_silu = sem("s_silu")
        s_gate = sem("s_gate")
        s_gru = sem("s_gru")
        s_gidx = sem("s_gidx")
        s_gat = [sem(f"s_gat{q}") for q in range(2)]
        s_nm = sem("s_nm")
        s_ss = sem("s_ss")
        s_nmr = sem("s_nmr")
        s_hn = sem("s_hn")
        s_msg = sem("s_msg")
        s_sidx = sem("s_sidx")
        s_sum = sem("s_sum")
        s_smc = sem("s_smc")
        s_sca = [sem(f"s_sca{q}") for q in range(2)]
        L = []
        for l in (1, 2):
            L.append(dict(
                row=[sem(f"t{l}_row{q}") for q in range(2)], same=sem(f"t{l}_same"), gidx=sem(f"t{l}_gidx"),
                gat=[sem(f"t{l}_gat{q}") for q in range(2)], sum=sem(f"t{l}_sum"), smc=sem(f"t{l}_smc"),
                sidx=sem(f"t{l}_sidx"), stage=sem(f"t{l}_stage"), sca=[sem(f"t{l}_sca{q}") for q in range(2)]))
        d_x = [[sem(f"d{l}_x{q}") for q in range(2)] for l in range(3)]
        d_a = [[sem(f"d{l}_a{q}") for q in range(2)] for l in range(3)]
        d_acc = [[sem(f"d{l}_acc{q}") for q in range(2)] for l in range(3)]
        d_used = sem("d_used")
        d_made = [sem(f"d{l}_made") for l in range(3)]
        d_out = [[sem(f"d{l}_out{q}") for q in range(2)] for l in range(3)]
        d_ch = {m: sem(f"d_ch{m}") for m in ("a", "b", "c", 1, 2)}
        d_req = {m: sem(f"d_req{m}") for m in "abc"}
        d_ans = {m: sem(f"d_ans{m}") for m in "abc"}
        d_deg = sem("d_deg")
        d_tot = sem("d_tot")
        d_h = sem("d_h")
        d_n = sem("d_n")
        d_xb = sem("d_xb")
        d_st = sem("d_st")
        d_h2 = sem("d_h2")
        d_gm = sem("d_gm")
        d_y = sem("d_y")
        d_yout = sem("d_yout")

        block = ctx.enter_context(nc.Block())

        def hold(eng, name, s, v):
            eng.wait_ge(s, v)
            eng.nop().then_inc(s_nop[name], 1)

        def rows_of(table, n, t):
            w = n * table.shape[1]
            return table[0:NP, :].rearrange("(p j) f -> p (j f)", p=P)[:, bass.ds(t * w, w)]

        ZR = 56

        def zero_table(eng, table, done):
            view = table[0:NP, :].rearrange("(p j) f -> p (j f)", p=P)
            w = ZR * table.shape[1]
            for c in range(J // ZR):
                eng.dma_start(view[:, c * w:(c + 1) * w], zero[:, 0:w]).then_inc(done, 16)
            eng.dma_start(table[NP:NP + P, :], zero[:, 0:table.shape[1]]).then_inc(done, 16)

        ZD = 16 * (J // ZR + 1)
        ZS = J // (NB // 2)

        def zero_slice(eng, l, i):
            w = ZS * H
            eng.dma_start(sums[l][1][0:NP, :].rearrange("(p j) f -> p (j f)", p=P)[:, bass.ds(i * w, w)],
                          zero[:, 0:w]).then_inc(s_zeroed[l], 16)

        def pair_of(buf, w):
            return buf[:].rearrange("p q j f -> p (q j f)")[:, 0:2 * JT * w]

        @block.sync
        def _(sp):
            def dense_0():
                def load(i):
                    sp.dma_start(pair_of(dx, H + 1), rows_of(xm, 2 * JT, i)).then_inc(d_x[0][0], 16)
                    sp.dma_start(pair_of(da, MW), rows_of(sums[0][0], 2 * JT, i)).then_inc(d_a[0][0], 16)

                def store(i):
                    hold(sp, "sp", d_made[0], i + 1)
                    o = pair_of(do, H)
                    sp.dma_start(rows_of(gtab[0], 2 * JT, i), o).then_inc(d_out[0][0], 16)
                    sp.dma_start(rows_of(sums[1][0], 2 * JT, i), o).then_inc(d_out[0][0], 16)

                def store_x1(i):
                    hold(sp, "sp", d_y, i * 2 + 2)
                    sp.dma_start(rows_of(x1tab, 2 * JT, i), pair_of(dy, H)).then_inc(d_yout, 16)

                def turn(i):
                    hold(sp, "sp", d_used, i + 1)
                    hold(sp, "sp", d_deg, i * 2 + 2)
                    hold(sp, "sp", d_xb, i * 2 + 2)
                    hold(sp, "sp", d_st, i * 2 + 2)
                    load(i + 1)
                    if not isinstance(i, int):
                        store(i - 1)
                    store_x1(i)

                load(0)
                turn(0)
                with sp.Fori(1, PAIRS - 1) as i:
                    turn(i)
                store(PAIRS - 2)
                store_x1(PAIRS - 1)
                store(PAIRS - 1)
                sp.wait_ge(d_yout, 16 * PAIRS)
                sp.wait_ge(d_out[0][0], 32 * PAIRS)

            def dense_12(l):
                def load(i, r):
                    q = r % 2
                    if l == 2:
                        sp.dma_start(pair_of((dh, dc)[q], H), rows_of(x1tab, 2 * JT, i * 2 + r)).then_inc(d_x[l][q], 16)
                    sp.dma_start(pair_of((da, dx)[q], H), rows_of(sums[l][0], 2 * JT, i * 2 + r)).then_inc(d_a[l][q], 16)

                def store(i, r):
                    q = r % 2
                    hold(sp, "sp", d_made[l], i * 2 + r + 1)
                    o = pair_of((do, dy)[q], H)
                    for table in ((gtab[1], sums[2][0]) if l == 1 else (out,)):
                        sp.dma_start(rows_of(table, 2 * JT, i * 2 + r), o).then_inc(d_out[l][q], 16)

                def turn(i, r):
                    store(i, r)
                    load(i, r + 2)

                load(0, 0)
                load(0, 1)
                with sp.Fori(0, (PAIRS - 2) // 2) as i:
                    turn(i, 0)
                    turn(i, 1)
                for r in range(2):
                    store((PAIRS - 2) // 2, r)
                for q in range(2):
                    sp.wait_ge(d_out[l][q], 16 * STORES[l] * PAIRS // 2)

            sp.dma_start(dsti[:], dst_col).then_inc(s_cols, 16)
            sp.dma_start(srci[:], src_col).then_inc(s_cols, 16)
            sp.dma_start(wcol[:], w_col).then_inc(s_cols, 16)
            sp.dma_start(ztab_i[:], types).then_inc(s_cols, 16)
            sp.wait_ge(s_zero, 1)
            for q in range(2):
                zero_table(sp, sums[0][q], s_zeroed[0])
            for l in (1, 2):
                for q in range(2):
                    sp.dma_start(sums[l][q][NP:NP + P, :], zero[:, 0:H]).then_inc(s_zeroed[l], 16)

            def load_batch(i, r):
                q = r % 2
                b = i * 2 + r
                cols = bass.ds(b * (U * P), U * P)
                sp.dma_start(srow[:, q, :], src_row[0:1, cols].to_broadcast([P, U * P])).then_inc(s_row[q], 16)
                sp.dma_start(drow[:, q, :], dst_row[0:1, cols].to_broadcast([P, U * P])).then_inc(s_row[q], 16)
                sp.dma_start(att[:, q, :], attrT[:, cols]).then_inc(s_att[q], 16)

            load_batch(0, 0)
            load_batch(0, 1)

            def prefetch(i, r):
                b = i * 2 + r
                hold(sp, "sp", s_same, b * U)
                hold(sp, "sp", s_hid, b * 2)
                load_batch(i, r + 1)

            with sp.Fori(0, (NB - 2) // 2) as i:
                prefetch(i, 1)
                prefetch(i, 2)
                zero_slice(sp, 1, i)
            zero_slice(sp, 1, (NB - 2) // 2)

            for l in range(3):
                if l > 0:
                    t = L[l - 1]

                    def load_rows(i, r, t=t):
                        q = r % 2
                        cols = bass.ds((i * 2 + r) * (U * P), U * P)
                        sp.dma_start(srow[:, q, :], src_row[0:1, cols].to_broadcast([P, U * P])).then_inc(t["row"][q], 16)

                    if l == 1:
                        sp.wait_ge(s_same, NB * U)
                    else:
                        sp.wait_ge(L[0]["same"], NB)
                    load_rows(0, 0)
                    load_rows(0, 1)
                    with sp.Fori(0, (NB - 2) // 2) as i:
                        for r in (1, 2):
                            hold(sp, "sp", t["same"], i * 2 + r)
                            load_rows(i, r + 1)
                        if l == 1:
                            zero_slice(sp, 2, i)
                    if l == 1:
                        zero_slice(sp, 2, (NB - 2) // 2)
                sca = s_sca if l == 0 else L[l - 1]["sca"]
                for q in range(2):
                    sp.wait_ge(sca[q], 16 * C // 2)

                if l == 0:
                    dense_0()
                else:
                    dense_12(l)

        @block.gpsimd
        def _(pool):
            pool.iota(iota_f[:], [[1, JZ]], base=0, channel_multiplier=0,
                      allow_small_or_imprecise_dtypes=True).then_inc(s_iota, 1)
            pool.iota(iota_b[:], [[1, NZ]], base=0, channel_multiplier=0,
                      allow_small_or_imprecise_dtypes=True).then_inc(s_iota, 1)
            pool.iota(part[:], [[0, 1]], base=0, channel_multiplier=1,
                      allow_small_or_imprecise_dtypes=True).then_inc(s_iota, 1)
            pool.iota(ncentre[:], [[0, 1]], base=-(JN - 1) // 2, channel_multiplier=-JN,
                      allow_small_or_imprecise_dtypes=True).then_inc(s_iota, 1)
            pool.memset(upto[:], 1.0).then_inc(s_iota, 1)
            pool.memset(ident[:], 0.0).then_inc(s_iota, 1)
            pool.wait_ge(s_iota, 6)
            pool.affine_select(out=upto[:], in_=upto[:], compare_op=ALU.is_ge, fill=0.0, base=0,
                               pattern=[[-1, P]], channel_multiplier=1).then_inc(s_iota, 1)
            pool.affine_select(out=ident[:], in_=ident[:], compare_op=ALU.not_equal, fill=1.0, base=0,
                               pattern=[[-1, P]], channel_multiplier=1).then_inc(s_iota, 1)

            def edge_pass(table, width, dst_tables, s_gi, s_g, rows, s_si, s_sm, s_sc, rows_free, zeroed):
                def gather(q, k):
                    pool.indirect_dma_start(rows[:, q, k, :], None, table,
                                            bass.IndirectOffsetOnAxis(gidx[:, q, k:k + 1], 0)).then_inc(s_g[q], 16)

                def scatter(i, r, k):
                    c = U * r + k
                    q = c % 2
                    before_it = i * U + c // 2
                    if isinstance(before_it, int):
                        if before_it > 0:
                            pool.wait_ge(s_sc[q], 16 * before_it)
                    else:
                        hold(pool, "pool", s_sc[q], before_it * 16)
                    pool.indirect_dma_start(dst_tables[q], bass.IndirectOffsetOnAxis(scidx[:, r % 2, k:k + 1], 0),
                                            sm[:, r % 2, k, 0:width], None, compute_op=ALU.add).then_inc(s_sc[q], 16)

                def ready(i, r):
                    b = i * 2 + r
                    hold(pool, "pool", s_gi, b + 1)
                    s_free, per = rows_free
                    if isinstance(b, int):
                        if b >= 2:
                            hold(pool, "pool", s_free, (b - 1) * per)
                    else:
                        hold(pool, "pool", s_free, (b - 1) * per)

                def sums_ready(i, r):
                    b = i * 2 + r
                    hold(pool, "pool", s_sm, b + 1)
                    hold(pool, "pool", s_si, b + 1)

                def step(i, r):
                    ready(i, r)
                    for k in range(U):
                        gather(r % 2, k)
                        if k == 0:
                            sums_ready(i, r - 2)
                        scatter(i, r - 2, k)

                for r in range(2):
                    ready(0, r)
                    for k in range(U):
                        gather(r, k)
                for s, v in zeroed:
                    pool.wait_ge(s, v)
                step(0, 2)
                step(0, 3)
                with pool.Fori(1, (NB - 2) // 2) as i:
                    step(i, 2)
                    step(i, 3)
                for r in range(2):
                    sums_ready((NB - 2) // 2, r)
                    for k in range(U):
                        scatter((NB - 2) // 2, r, k)

            def accumulate(l):
                def step(i, r):
                    q = r % 2
                    hold(pool, "pool", d_a[l][q], (half(i, r) + 1) * 16)
                    for m in range(2):
                        pool.dma_start(pair_of((da, dx)[q], H)[:, m * JT * H:(m + 1) * JT * H],
                                       rows_of(sums[l][1], JT, i * 4 + (2 * r + m)),
                                       accum_op=ALU.add).then_inc(d_acc[l][q], 16)
                in_pairs(pool, PAIRS, step)

            def dense_0():
                def add_sums(i):
                    hold(pool, "pool", d_a[0][0], i * 16 + 16)
                    for m in range(2):
                        pool.dma_start(pair_of(da, MW)[:, m * JT * MW:(m + 1) * JT * MW],
                                       rows_of(sums[0][1], JT, i * 2 + m), accum_op=ALU.add).then_inc(d_acc[0][0], 16)

                def row_like(v):
                    return v.unsqueeze(1).to_broadcast([P, JT, H])

                def step(i, last=False):
                    for q in range(2):
                        pool.wait_ge(d_x[0][0], i * 16 + 16)
                        if not isinstance(i, int) or i > 0:
                            pool.wait_ge(d_y, i * 2)
                        pool.tensor_tensor(xb[:, q, :, :], dx[:, q, :, 0:H], row_like(bet[:]), ALU.add).then_inc(d_xb, 1)
                    for q in range(2):
                        pool.wait_ge(d_tot, i + 1)
                        if not isinstance(i, int) or i > 0:
                            pool.wait_ge(d_n, i * 2)
                        pool.tensor_tensor(st[:, q, :, :], da[:, q, :, 0:H],
                                           itot[:, q, :].unsqueeze(2).to_broadcast([P, JT, H]), ALU.mult).then_inc(d_st, 1)
                    for q in range(2):
                        pool.wait_ge(d_h, i * 2 + q + 1)
                        pool.wait_ge(d_st, i * 2 + q + 1)
                        pool.tensor_tensor(st[:, q, :, :], dh[:, q, :, :], st[:, q, :, :], ALU.add).then_inc(d_h2, 1)
                    if not last:
                        add_sums(i + 1)
                    for q in range(2):
                        pool.wait_ge(d_n, i * 2 + q + 1)
                        pool.tensor_tensor(dh[:, q, :, :], dh[:, q, :, :], row_like(gam[:]), ALU.mult).then_inc(d_gm, 1)
                    for q in range(2):
                        pool.wait_ge(d_gm, i * 2 + q + 1)
                        if not isinstance(i, int) or i > 0:
                            pool.wait_ge(d_yout, i * 16)
                            pool.wait_ge(d_made[0], i)
                        pool.tensor_tensor(dy[:, q, :, :], dh[:, q, :, :], xb[:, q, :, :], ALU.add).then_inc(d_y, 1)

                add_sums(0)
                step(0)
                with pool.Fori(1, PAIRS - 1) as i:
                    step(i)
                step(PAIRS - 1, last=True)

            edge_pass(xm, MW, sums[0], s_gidx, s_gat, xg, s_sidx, s_smc, s_sca, (s_msg, 1), [(s_zeroed[0], 2 * ZD)])
            for q in range(2):
                pool.wait_ge(s_sca[q], 16 * C // 2)
            dense_0()
            for l in (1, 2):
                t = L[l - 1]
                if l == 1:
                    pool.wait_ge(d_out[0][0], 32 * PAIRS)
                else:
                    for q in range(2):
                        pool.wait_ge(d_out[1][q], 16 * STORES[1] * PAIRS // 2)
                edge_pass(gtab[l - 1], H, sums[l], t["gidx"], t["gat"], gx, t["sidx"], t["smc"], t["sca"],
                          (t["sum"], 1), [(s_zeroed[l], 16 * (NB // 2) + 32)])
                for q in range(2):
                    pool.wait_ge(t["sca"][q], 16 * C // 2)
                accumulate(l)

        @block.scalar
        def _(act):
            act.dma_start(w1T_s[:], w1T).then_inc(s_const, 16)
            act.dma_start(b1_s[:], b1).then_inc(s_const, 16)
            act.dma_start(w2_s[0:H, :], w2T).then_inc(s_const, 16)
            act.dma_start(w2_s[H:H + 1, :], b2).then_inc(s_const, 16)
            act.dma_start(embT_s[:], embT).then_inc(s_const, 16)
            act.dma_start(adT_s[:], adaptT).then_inc(s_const, 16)
            act.dma_start(gam[:], gamma.to_broadcast([P, H])).then_inc(s_const, 16)
            act.dma_start(bet[:], beta.to_broadcast([P, H])).then_inc(s_const, 16)
            act.wait_ge(s_iota, 8)
            act.activation(identf[:], ident[:], ACT.Copy).then_inc(s_uc, 1)
            act.wait_ge(s_u, 1)
            act.activation(u_s[:], p_v[0:G, 0, 0:NZ], ACT.Copy).then_inc(s_uc, 1)
            act.wait_ge(s_u, 2)
            act.activation(tt_s[:], p_v[0:NZ, 1, 0:NZ], ACT.Copy).then_inc(s_uc, 1)
            act.wait_ge(s_arg, 1)
            act.activation(t1[:, 1, :], t1[:, 0, :], ACT.Sin, scale=PI / (2 * CUTOFF)).then_inc(s_sin, 1)

            def distances(i, r):
                q = r % 2
                b = i * 2 + r
                act.wait_ge(s_row[q], (half(i, r) + 1) * 32)
                if not isinstance(b, int) or b > 0:
                    act.wait_ge(s_mask, b * 2)
                for w, rows in enumerate((srow, drow)):
                    act.activation(dist[:, w, :], rows[:, q, :], ACT.Abs, bias=ncentre[:, 0:1]).then_inc(s_dist, 1)

            def hidden(i, r, m):
                b = i * 2 + r
                act.wait_ge(s_hid, b * 2 + m + 1)
                if m == 0 and (not isinstance(b, int) or b > 0):
                    act.wait_ge(s_gate, b)
                act.activation(hT[0:H, m * (U * P // 2):(m + 1) * (U * P // 2)], p_h[:, 0:U * P // 2],
                               ACT.Silu, bias=b1_s[:, 0:1]).then_inc(s_silu, 1)

            def step(i, r):
                q = r % 2
                b = i * 2 + r
                first = isinstance(b, int) and b == 0
                act.wait_ge(s_nm, b + 1)
                for k in range(U):
                    last = act.activation(sq[:, k, :], xg[:, q, k, 0:H], ACT.Square, bias=nm[:, k:k + 1],
                                          accum_out=ss[:, k:k + 1])
                last.then_inc(s_ss, 1)
                act.wait_ge(s_ss, b * 2 + 1)
                act.activation(sd[:], ss[:], ACT.Sqrt, scale=1.0 / H, bias=epsc[:, 0:1]).then_inc(s_ss, 1)
                hidden(i, r, 0)
                hidden(i, r, 1)
                act.wait_ge(s_nmr, b + 1)
                if not first:
                    act.wait_ge(s_msg, b)
                for k in range(U):
                    last = act.activation(hn[:, k, :], xg[:, q, k, 0:H], ACT.Relu, bias=nmr[:, k:k + 1],
                                          scale=rs[:, k:k + 1])
                last.then_inc(s_hn, 1)
                act.wait_ge(s_tr, b + 1)
                if not first:
                    act.wait_ge(s_tv, b * 2)
                act.activation(ohT[:], p_t[:], ACT.Copy).then_inc(s_trc, 1)
                if not (isinstance(i, int) and b == NB - 1):
                    distances(i, r + 1)
                copy_sums(i, r, s_sum, s_smc, s_sca, MW)

            def copy_sums(i, r, s_sum, s_smc, s_sca, w):
                b = i * 2 + r
                act.wait_ge(s_sum, b + 1)
                if not isinstance(b, int) or b >= 2:
                    landed(act, i, r, s_sca)
                act.activation(sm[:, r % 2, :, 0:w], p_s[:, :, 0:w], ACT.Copy).then_inc(s_smc, 1)

            act.wait_ge(s_iota, 8)
            act.wait_ge(s_const, 8 * 16)
            act.wait_ge(s_set, SETUP)
            distances(0, 0)
            in_pairs(act, NB, step)

            def norm(m, i):
                for q in range(2):
                    act.wait_ge(d_req[m], i * 4 + q + 1)
                    act.activation(dq[:, q, :, :], dc[:, q, :, :], ACT.Square).then_inc(d_ans[m], 1)
                for q in range(2):
                    act.wait_ge(d_req[m], i * 4 + q + 3)
                    act.activation(rroot[:, q, :], rsq[:, q, :], ACT.Sqrt, scale=1.0 / H, bias=epsc[:, 0:1]).then_inc(d_ans[m], 1)

            def dense_step(i):
                norm("a", i)
                act.wait_ge(d_acc[0][0], i * 32 + 32)
                if not isinstance(i, int) or i > 0:
                    act.wait_ge(d_used, i)
                for q in range(2):
                    act.activation(rdeg[:, q, :], da[:, q, :, H + 1], ACT.Sqrt, bias=1.0).then_inc(d_deg, 1)
                if not isinstance(i, int) or i > 0:
                    norm("c", i - 1)
                norm("b", i)

            dense_step(0)
            with act.Fori(1, PAIRS) as i:
                dense_step(i)
            norm("c", PAIRS - 1)
            for l in (1, 2):
                t = L[l - 1]
                in_pairs(act, NB, lambda i, r: copy_sums(i, r, t["sum"], t["smc"], t["sca"], H))

        @block.tensor
        def _(pe):
            pe.wait_ge(s_const, 8 * 16)
            pe.matmul(p_v[0:G, 0, 0:NZ], adT_s[:], embT_s[:], start=True, stop=True).then_inc(s_u, 1)
            pe.wait_ge(s_uc, 2)
            pe.matmul(p_v[0:NZ, 1, 0:NZ], u_s[:], embT_s[:], start=True, stop=True).then_inc(s_u, 1)
            pe.wait_ge(s_uc, 3)
            pe.wait_ge(s_set, SETUP)

            def step(i, r):
                q = r % 2
                b = i * 2 + r
                first = isinstance(b, int) and b == 0
                hold(pe, "pe", s_att[q], (half(i, r) + 1) * 16)
                hw = U * P // 2

                def hidden(m):
                    if not (first and m == 0):
                        hold(pe, "pe", s_silu, b * 2 + m)
                    pe.matmul(p_h[:, 0:hw], w1T_s[:], att[:, q, m * hw:(m + 1) * hw], start=True, stop=True).then_inc(s_hid, 1)

                hidden(0)
                pe.wait_ge(s_mask, b * 2 + 2)
                for k in range(U):
                    for w in range(2):
                        if not (first and k == 0):
                            pe.wait_ge(s_zr, b * (2 * U) + 2 * k + w - 1)
                        for m in range(NPACK):
                            last = pe.matmul(p_z[:, w, 0:JZ], mask[:, w, k * P:(k + 1) * P], ztab[:, m, :],
                                             start=(m == 0), stop=(m == NPACK - 1))
                        last.then_inc(s_zp, 1)
                hidden(1)
                pe.wait_ge(s_silu, b * 2 + 2)
                if not first:
                    pe.wait_ge(s_gru, b)
                for k in range(U):
                    last = pe.matmul(p_g[:, k, :], hT[:, k * P:(k + 1) * P], w2_s[:], start=True, stop=True)
                last.then_inc(s_gate, 1)
                pe.wait_ge(s_oh, b + 1)
                if not first:
                    pe.wait_ge(s_trc, b)
                for k in range(U):
                    last = pe.transpose(p_t[:, k * P:(k + 1) * P], oh[:, k, :], ident[:])
                last.then_inc(s_tr, 1)
                pe.wait_ge(s_trc, b + 1)
                for g, ks in enumerate(GROUPS):
                    if not first:
                        pe.wait_ge(s_ad, (b - 1) * U + ks[-1] + 1)
                    for k in ks:
                        last = pe.matmul(p_v[:, k, 0:NZ], ohT[:, k * P:(k + 1) * P], tt_s[:], start=True, stop=True)
                    last.then_inc(s_tv, 1)
                sum_batch(i, r, msg, MW, s_msg, s_sum, s_smc)

            def sum_batch(i, r, rows, w, s_rows, s_sum, s_smc):
                b = i * 2 + r
                first = isinstance(b, int) and b == 0
                pe.wait_ge(s_rows, b + 1)
                if not first:
                    pe.wait_ge(s_smc, b)
                for k in range(U):
                    last = pe.matmul(p_s[:, k, 0:w], same[:, r % 2, k, :], rows[:, k, :], start=True, stop=True)
                last.then_inc(s_sum, 1)

            in_pairs(pe, NB, step)

            for l in (1, 2):
                t = L[l - 1]

                def step(i, r):
                    q = r % 2
                    pe.wait_ge(t["gat"][q], (half(i, r) + 1) * (16 * U))
                    sum_batch(i, r, gx[:, q, :, :], H, t["same"], t["sum"], t["smc"])
                in_pairs(pe, NB, step)

        @block.vector
        def _(dve):
            dve.memset(zero[:], 0.0).then_inc(s_zero, 1)
            n = [0]

            def do_(ins):
                n[0] += 1
                ins.then_inc(s_set, 1)
                dve.wait_ge(s_set, n[0])

            do_(dve.memset(hT[:], 1.0))
            do_(dve.memset(msg[:], 1.0))
            do_(dve.memset(epsc[:], EPS))
            do_(dve.memset(ones[:], 1.0))
            dve.wait_ge(s_iota, 8)
            dve.wait_ge(s_cols, 64)
            do_(dve.tensor_scalar(t0[:, 0, :], wcol[:], 1.0 / (2 * CUTOFF), ROUND, ALU.mult, ALU.add))
            do_(dve.tensor_scalar(t0[:, 1, :], t0[:, 0, :], -ROUND, None, ALU.add))
            n[0] += 1
            dve.scalar_tensor_tensor(t1[:, 0, :], t0[:, 1, :], -2.0 * CUTOFF, wcol[:], ALU.mult, ALU.add).then_inc(s_arg, 1)
            n[0] -= 1
            for m in range(NPACK):
                do_(dve.tensor_scalar(ztab[:, m, :], ztab_i[:, m * JZ:(m + 1) * JZ], float(128 ** m), None, ALU.mult))
            do_(dve.tensor_copy(srcf[:], srci[:]))
            do_(dve.tensor_copy(ec[:, :, ESRC], srcf[:]))
            do_(dve.tensor_scalar(npp[:, 0:1], part[:], float(NP), None, ALU.add))
            do_(dve.tensor_scalar(ec[:, :, SPARE], srcf[:], -1.0, npp[:, 0:1], ALU.mult, ALU.add))
            do_(dve.tensor_tensor(ec[:, :, BASE], srcf[:], ec[:, :, SPARE], ALU.subtract))
            dve.wait_ge(s_sin, 1)
            do_(dve.tensor_tensor(t0[:, 0, :], t1[:, 1, :], t1[:, 1, :], ALU.mult))
            do_(dve.tensor_scalar(t0[:, 1, :], t0[:, 0, :], -1.0, 1.0, ALU.mult, ALU.add))
            do_(dve.scalar_tensor_tensor(ec[:, :, CUT], wcol[:], CUTOFF, t0[:, 1, :], ALU.is_lt, ALU.mult))
            for w, idx in enumerate((srci[:], dsti[:, 0:C])):
                do_(dve.tensor_scalar(t0[:, 0, :], idx, 0.5, 1.0 / JN, ALU.add, ALU.mult))
                do_(dve.tensor_scalar(t0[:, 1, :], t0[:, 0, :], -0.5, ROUND, ALU.add, ALU.add))
                do_(dve.tensor_scalar(t0[:, 0, :], t0[:, 1, :], -ROUND, None, ALU.add))
                do_(dve.scalar_tensor_tensor(t1[:, 0, :], t0[:, 0, :], -float(JN), idx, ALU.mult, ALU.add))
                do_(dve.tensor_scalar(t2[:, 0, :], t1[:, 0, :], float(JZ), None, ALU.is_ge))
                do_(dve.scalar_tensor_tensor(t2[:, 1, :], t1[:, 0, :], float(2 * JZ), t2[:, 0, :], ALU.is_ge, ALU.add))
                do_(dve.scalar_tensor_tensor(ec[:, :, CSRC + w], t2[:, 1, :], -float(JZ), t1[:, 0, :], ALU.mult, ALU.add))
                do_(dve.tensor_scalar(shi[:, :, w], t2[:, 1, :], 7.0, None, ALU.mult))
            for r in range(2):
                dve.tensor_copy(gidx[:, r, :], dsti[:, r * U:(r + 1) * U]).then_inc(s_gidx, 1)
            assert n[0] == SETUP, n[0]

            count = [0]

            def step(i, r):
                q = r % 2
                b = i * 2 + r
                first = isinstance(b, int) and b == 0
                count[0] = 0

                def chain(ins):
                    count[0] += 1
                    ins.then_inc(s_chain, 1)
                    return count[0]

                def after(v):
                    dve.wait_ge(s_chain, b * CHAIN + v)

                cols = bass.ds(b * U, U)
                chain(dve.tensor_copy(bc[:], ec[:, cols, :]))
                v_bc = chain(dve.tensor_copy(bsh[:], shi[:, cols, :]))
                for w in range(2):
                    dve.wait_ge(s_dist, b * 2 + w + 1)
                    if not first:
                        dve.wait_ge(s_zp, b * (2 * U))
                    dve.tensor_scalar(mask[:, w, :], dist[:, w, :], JN / 2, None, ALU.is_lt).then_inc(s_mask, 1)
                dve.wait_ge(s_gat[q], (half(i, r) + 1) * (16 * U))
                after(chain(dve.reduce_sum(sx[:], xg[:, q, :, 0:H], axis=AX)))
                dve.tensor_scalar(nm[:], sx[:], -1.0 / H, None, ALU.mult).then_inc(s_nm, 1)
                if not (isinstance(b, int) and b == NB - 1):
                    dve.tensor_copy(gidx[:, q, :], dsti[:, bass.ds(b * U + 2 * U, U)]).then_inc(s_gidx, 1)
                for k in range(U):
                    for w in range(2):
                        dve.wait_ge(s_zp, b * (2 * U) + 2 * k + w + 1)
                        dve.scalar_tensor_tensor(junk[:, w, :], iota_f[:], bc[:, k, w:w + 1], p_z[:, w, 0:JZ], ALU.is_equal,
                                                 ALU.mult, accum_out=zq[:, k, w:w + 1]).then_inc(s_zr, 1)
                dve.wait_ge(s_zr, (b + 1) * (2 * U))
                after(chain(dve.tensor_copy(zi[:], zq[:])))
                dve.wait_ge(s_ss, (b + 1) * 2)
                chain(dve.reciprocal(rs[:], sd[:]))
                after(chain(dve.tensor_tensor(zi2[:], zi[:], bsh[:], ALU.logical_shift_right)))
                dve.tensor_tensor(nmr[:], nm[:], rs[:], ALU.mult).then_inc(s_nmr, 1)
                after(chain(dve.tensor_scalar(zi3[:], zi2[:], 127, None, ALU.bitwise_and)))
                after(chain(dve.tensor_copy(zf[:], zi3[:])))
                if not first:
                    dve.wait_ge(s_tr, b)
                for k in range(U):
                    last = dve.tensor_scalar(oh[:, k, :], iota_b[:], zf[:, k, 1:2], None, ALU.is_equal)
                last.then_inc(s_oh, 1)
                dve.wait_ge(s_row[q], (half(i, r) + 1) * 32)
                if not isinstance(b, int) or b >= 2:
                    dve.wait_ge(s_sum, b - 1)
                for k in range(U):
                    dve.scalar_tensor_tensor(same[:, q, k, :], srow[:, q, k * P:(k + 1) * P],
                                             bc[:, k, ESRC:ESRC + 1], upto[:], ALU.is_equal, ALU.mult,
                                             accum_out=dup[:, k:k + 1]).then_inc(s_same, 1)
                chain(dve.tensor_tensor(cw[:], bc[:, :, CUT], xg[:, q, :, H], ALU.mult))
                dve.wait_ge(s_same, (b + 1) * U)
                after(chain(dve.scalar_tensor_tensor(dupn[:], dup[:], 2.0, bc[:, :, SPARE], ALU.min, ALU.mult)))
                chain(dve.tensor_tensor(sidx[:, cols], dupn[:], bc[:, :, BASE], ALU.add))
                if not isinstance(b, int) or b >= 2:
                    landed(dve, i, r, s_sca)
                dve.tensor_tensor(scidx[:, q, :], dupn[:], bc[:, :, BASE], ALU.add).then_inc(s_sidx, 1)
                if not first:
                    dve.wait_ge(s_sum, b)
                chain(dve.tensor_copy(msg[:, :, H], xg[:, q, :, H]))
                for k in range(U):
                    if k in (GROUPS[0][0], GROUPS[1][0]):
                        dve.wait_ge(s_tv, b * 2 + (1 if k == 0 else 2))
                    dve.scalar_tensor_tensor(junka[:, k, :], iota_f[:, 0:NZ], zf[:, k, 0:1], p_v[:, k, 0:NZ],
                                             ALU.is_equal, ALU.mult, accum_out=adap[:, k:k + 1]).then_inc(s_ad, 1)
                dve.wait_ge(s_gate, b + 1)
                dve.wait_ge(s_ad, (b + 1) * U)
                dve.tensor_tensor(gg[:], p_g[:], adap[:].unsqueeze(2).to_broadcast([P, U, H]), ALU.add).then_inc(s_gru, 1)
                dve.wait_ge(s_gru, b + 1)
                after(chain(dve.tensor_tensor(gw[:], gg[:], cw[:].unsqueeze(2).to_broadcast([P, U, H]), ALU.mult)))
                dve.wait_ge(s_hn, b + 1)
                dve.tensor_tensor(msg[:, :, 0:H], hn[:], gw[:], ALU.mult).then_inc(s_msg, 1)
                assert count[0] == CHAIN, count[0]

            in_pairs(dve, NB, step)

            def wide(v):
                return v.unsqueeze(2).to_broadcast([P, JT, H])

            class Steps:

                def __init__(self, m, base):
                    self.m, self.base, self.n = m, base, 0

                def __call__(self, ins):
                    self.n += 1
                    ins.then_inc(d_ch[self.m], 1)

                def done(self, k=None):
                    dve.wait_ge(d_ch[self.m], self.base + (self.n if k is None else k))

            def deviation(m, i, rows, step):
                first = step.n
                for q in range(2):
                    step(dve.reduce_sum(rsum[:, q, :], rows(q), axis=AX))
                for q in range(2):
                    step.done(first + q + 1)
                    dve.scalar_tensor_tensor(dc[:, q, :, :], wide(rsum[:, q, :]), -1.0 / H, rows(q), ALU.mult,
                                             ALU.add).then_inc(d_req[m], 1)
                for q in range(2):
                    dve.wait_ge(d_ans[m], i * 4 + q + 1)
                    dve.reduce_sum(rsq[:, q, :], dq[:, q, :, :], axis=AX).then_inc(d_req[m], 1)

            def inverse(m, i, step):
                for q in range(2):
                    dve.wait_ge(d_ans[m], i * 4 + q + 3)
                    step(dve.reciprocal(rinv[m][:, q, :], rroot[:, q, :]))

            def stage_a(i):
                later = not isinstance(i, int) or i > 0
                step = Steps("a", i * CHAIN_D["a"])
                dve.wait_ge(d_x[0][0], i * 16 + 16)
                deviation("a", i, lambda q: dx[:, q, :, 0:H], step)
                dve.wait_ge(d_acc[0][0], i * 32 + 32)
                step(dve.tensor_scalar(rtot[:], da[:, :, :, H], 1e-8, None, ALU.max))
                step.done()
                if later:
                    dve.wait_ge(d_st, i * 2)
                dve.reciprocal(itot[:], rtot[:]).then_inc(d_tot, 1)
                inverse("a", i, step)
                if later:
                    dve.wait_ge(d_y, i * 2)
                for q in range(2):
                    step.done(step.n - 1 + q)
                    dve.scalar_tensor_tensor(dh[:, q, :, :], dc[:, q, :, :], 0.0, wide(rinv["a"][:, q, :]), ALU.max,
                                             ALU.mult).then_inc(d_h, 1)
                dve.wait_ge(d_deg, i * 2 + 2)
                step(dve.reciprocal(dinv[:, bass.ds(i * (2 * JT), 2 * JT)], rdeg[:].rearrange("p q j -> p (q j)")))
                step.done()
                dve.nop().then_inc(d_used, 1)
                assert step.n == CHAIN_D["a"], step.n

            def stage_b(i):
                step = Steps("b", i * CHAIN_D["b"])
                dve.wait_ge(d_h2, i * 2 + 2)
                deviation("b", i, lambda q: st[:, q, :, :], step)
                inverse("b", i, step)
                for q in range(2):
                    step.done(step.n - 1 + q)
                    dve.tensor_tensor(dh[:, q, :, :], dc[:, q, :, :], wide(rinv["b"][:, q, :]), ALU.mult).then_inc(d_n, 1)
                assert step.n == CHAIN_D["b"], step.n

            def stage_c(i):
                step = Steps("c", i * CHAIN_D["c"])
                dve.wait_ge(d_y, i * 2 + 2)
                if not isinstance(i, int) or i > 0:
                    dve.wait_ge(d_out[0][0], i * 32)
                deviation("c", i, lambda q: dy[:, q, :, :], step)
                inverse("c", i, step)
                step.done()
                step(dve.tensor_tensor(fac[:], rinv["c"][:].rearrange("p q j -> p (q j)"),
                                       dinv[:, bass.ds(i * (2 * JT), 2 * JT)], ALU.mult))
                step.done()
                for q in range(2):
                    last = dve.scalar_tensor_tensor(do[:, q, :, :], dc[:, q, :, :], 0.0,
                                                    wide(fac[:, q * JT:(q + 1) * JT]), ALU.max, ALU.mult)
                last.then_inc(d_made[0], 1)
                assert step.n == CHAIN_D["c"], step.n

            stage_a(0)
            stage_b(0)
            with dve.Fori(1, PAIRS) as i:
                stage_a(i)
                stage_c(i - 1)
                stage_b(i)
            stage_c(PAIRS - 1)

            def dense(l):
                def rows(buf):
                    return pair_of(buf, H).rearrange("p (j f) -> p j f", f=H)

                def wide2(v):
                    return v.unsqueeze(2).to_broadcast([P, 2 * JT, H])

                def pair(i, r):
                    q = r % 2
                    b = i * 2 + r
                    step = Steps(l, b * CHAIN_D[l])
                    if not isinstance(b, int) or b > 0:
                        dve.wait_ge(d_made[l], b)
                    step(dve.tensor_tensor(fac[:], dinv[:, bass.ds(b * (2 * JT), 2 * JT)], ones[:], ALU.mult))
                    step.done()
                    if l == 1:
                        step(dve.tensor_tensor(fac2[:], fac[:], fac[:], ALU.mult))
                    dve.wait_ge(d_acc[l][q], (half(i, r) + 1) * 32)
                    if not isinstance(b, int) or b >= 2:
                        dve.wait_ge(d_out[l][q], half(i, r) * (16 * STORES[l]))
                    if l == 1:
                        step.done()
                        dve.tensor_tensor(rows((do, dy)[q]), rows((da, dx)[q]), wide2(fac2[:]), ALU.mult).then_inc(d_made[l], 1)
                    else:
                        step(dve.tensor_tensor(rows((dq, st)[q]), rows((da, dx)[q]), wide2(fac[:]), ALU.mult))
                        step.done()
                        dve.wait_ge(d_x[l][q], (half(i, r) + 1) * 16)
                        dve.tensor_tensor(rows((do, dy)[q]), rows((dq, st)[q]), rows((dh, dc)[q]), ALU.add).then_inc(d_made[l], 1)
                    assert step.n == CHAIN_D[l], step.n
                in_pairs(dve, PAIRS, pair)

            for l in (1, 2):
                t = L[l - 1]
                for r in range(2):
                    dve.tensor_copy(gidx[:, r, :], dsti[:, r * U:(r + 1) * U]).then_inc(t["gidx"], 1)

                def step(i, r):
                    q = r % 2
                    b = i * 2 + r
                    cols = bass.ds(b * U, U)
                    if not isinstance(b, int) or b > 0:
                        hold(dve, "dve", t["same"], b)
                    dve.tensor_copy(bc[:, :, 0], srcf[:, cols]).then_inc(t["stage"], 1)
                    dve.wait_ge(t["stage"], b + 1)
                    dve.wait_ge(t["row"][q], (half(i, r) + 1) * 16)
                    if not isinstance(b, int) or b >= 2:
                        dve.wait_ge(t["sum"], b - 1)
                    for k in range(U):
                        last = dve.tensor_scalar(same[:, q, k, :], srow[:, q, k * P:(k + 1) * P], bc[:, k, 0:1], None, ALU.is_equal)
                    last.then_inc(t["same"], 1)
                    if not isinstance(b, int) or b >= 2:
                        landed(dve, i, r, t["sca"])
                        hold(dve, "dve", t["sidx"], b)
                    dve.tensor_copy(scidx[:, q, :], sidx[:, cols]).then_inc(t["sidx"], 1)
                    if not (isinstance(b, int) and b == NB - 1):
                        hold(dve, "dve", t["gat"][q], (half(i, r) + 1) * (16 * U))
                        dve.tensor_copy(gidx[:, q, :], dsti[:, bass.ds(b * U + 2 * U, U)]).then_inc(t["gidx"], 1)
                in_pairs(dve, NB, step)
                dense(l)


def kernel(x, src, dst, edge_attr_40, edge_weight, node_type_119, node_vec, L0_gnn_W1, L0_gnn_b1, L0_gnn_W2,
           L0_gnn_b2, L0_gnn_emb, L0_gnn_adaptW, L0_gnn_gamma, L0_gnn_beta):
    import numpy as np
    import concourse.bacc as bacc
    from concourse.bass_utils import run_bass_kernel_spmd

    def padded(a, n, fill=0):
        a = np.asarray(a)
        out = np.zeros((n,) + a.shape[1:], a.dtype)
        out[:a.shape[0]] = a
        if not isinstance(fill, int):
            out[a.shape[0]:] = fill
        return out

    spare = (NP + np.arange(E) % P).astype(np.int32)[np.asarray(src).shape[0]:]
    srcp = padded(src, E, spare)
    dstp = padded(dst, E)

    def by_chunk(a):
        return np.ascontiguousarray(a.reshape(C, P).T)

    arrays = {
        "xm": padded(np.concatenate([np.asarray(x), np.asarray(node_vec)[:, None]], axis=1), NP),
        "src_col": by_chunk(srcp),
        "dst_col": np.concatenate([by_chunk(dstp), np.zeros((P, 2 * U), dstp.dtype)], axis=1),
        "w_col": by_chunk(padded(edge_weight, E)),
        "src_row": srcp[None, :],
        "dst_row": dstp[None, :],
        "attrT": np.ascontiguousarray(padded(edge_attr_40, E).T),
        "types": padded(node_type_119, P * JN).reshape(P, JN),
        "w1T": np.ascontiguousarray(np.asarray(L0_gnn_W1).T),
        "b1": np.asarray(L0_gnn_b1)[:, None],
        "w2T": np.ascontiguousarray(np.asarray(L0_gnn_W2).T),
        "b2": np.asarray(L0_gnn_b2)[None, :],
        "embT": np.ascontiguousarray(np.asarray(L0_gnn_emb).T),
        "adaptT": np.ascontiguousarray(np.asarray(L0_gnn_adaptW).T),
        "gamma": np.asarray(L0_gnn_gamma)[None, :],
        "beta": np.asarray(L0_gnn_beta)[None, :],
    }
    nc = bacc.Bacc("TRN2", target_bir_lowering=False, num_devices=1)
    args = [nc.dram_tensor(k, a.shape, mybir.dt.from_np(a.dtype), kind="ExternalInput").ap() for k, a in arrays.items()]
    args.append(nc.dram_tensor("result", (NP, H), F32, kind="ExternalOutput").ap())
    build(nc, *args)
    got = run_bass_kernel_spmd(nc, [arrays], core_ids=[0])
    return got.results[0]["result"][:N]
```

```python
from contextlib import ExitStack

import concourse.bass as bass
from concourse import mybir

F32 = mybir.dt.float32
I32 = mybir.dt.int32
BF16 = mybir.dt.bfloat16
F16 = mybir.dt.float16
ALU = mybir.AluOpType
ACT = mybir.ActivationFunctionType
AX = mybir.AxisListType.X

P = 128
N = 100000
H = 48
R = 40
NZ = 119
G = 32
J = 784
NP = P * J
NPACK = 3
LOW = 11
JZ = 261
JN = JZ * NPACK
U = 7
C = 392
NB = C // U
E = C * P
GROUPS = (range(0, 4), range(4, 7))
MW = H + 2
JT = 28
NT = J // JT
CUTOFF = 6.0
EPS = 1e-5
PI = 3.141592653589793
ROUND = 12582912.0
assert NP >= N and P * JN >= N and NB % 2 == 0 and JT * NT == J and NT % 2 == 0
CSRC, CDST, ESRC, SPARE, BASE, CUT = range(6)
NF = 6


def in_pairs(eng, n, step, last_two=False):
    for r in range(3):
        step(0, r)
    pairs = (n - 1) // 2 - last_two
    with eng.Fori(1, pairs) as i:
        step(i, 1)
        step(i, 2)
    step(pairs, 1)
    if last_two:
        step(pairs, 2)
        step(pairs, 3)


LAG = 3
SETUP = 41
CHAIN_X = 8
CHAIN_Y = 5
CHAIN_D = {"a": 6, "b": 4, "c": 5, 1: 2, 2: 2}
PAIRS = NT // 2
STORES = (3, 2, 1)


def landed(eng, i, r, s_sca):
    chunks = U * (r - 1)
    for q in range(2):
        eng.wait_ge(s_sca[q], (i * U + (chunks + 1 - q) // 2) * 16)


def half(i, r):
    return i + r // 2


def build(nc, xm, src_col, dst_col, w_col, src_row, dst_row, attrT, types, w1T, b1, w2T, b2, embT,
          adaptT, gamma, beta, out):
    ctx = ExitStack()
    with ctx:
        def sb(name, shape, dt=F32):
            return ctx.enter_context(nc.sbuf_tensor(name, shape, dt))

        def ps(name, shape, dt=F32):
            return ctx.enter_context(nc.psum_tensor(name, shape, dt))

        def sem(name):
            return ctx.enter_context(nc.semaphore(name))

        def dram(name, rows, width):
            return nc.dram_tensor(name, [rows, width], F32, kind="Internal").ap()

        sums = [[dram(f"sums{l}_{q}", NP + P, MW if l == 0 else H) for q in range(2)] for l in range(3)]
        gtab = [dram(f"gtab{l}", NP, H) for l in range(2)]
        x1tab = dram("x1tab", NP, H)

        zero = sb("zero", [P, 56 * MW])
        ident = sb("ident", [P, P], BF16)
        identf = sb("identf", [P, P])
        upto = sb("upto", [P, P])
        iota_f = sb("iota_f", [P, JZ])
        iota_b = sb("iota_b", [P, NZ], BF16)
        part = sb("part", [P, 1])
        ncentre = sb("ncentre", [P, 1])
        epsc = sb("epsc", [P, 1])
        w1T_s = sb("w1T_s", [R, H])
        b1_s = sb("b1_s", [H, 1])
        w2_s = sb("w2_s", [H + 1, H])
        embT_s = sb("embT_s", [G, NZ])
        adT_s = sb("adT_s", [G, G])
        u_s = sb("u_s", [G, NZ])
        tt_s = sb("tt_s", [NZ, NZ])
        tt_b = sb("tt_b", [NZ, 3, NZ], BF16)
        tt_r = sb("tt_r", [NZ, 2, NZ])
        gam = sb("gam", [P, H])
        bet = sb("bet", [P, H])
        ztab_i = sb("ztab_i", [P, JN], I32)
        ztab = sb("ztab", [P, 2, JZ], F16)
        dsti = sb("dsti", [P, C + 2 * U], I32)
        srci = sb("srci", [P, C], I32)
        srcf = sb("srcf", [P, C])
        wcol = sb("wcol", [P, C])
        st = sb("st", [P, 2, JT, H])
        flat = st[:].rearrange("p q j f -> p (q j f)")
        t0, t1, t2 = (flat[:, m * 2 * C:(m + 1) * 2 * C].rearrange("p (a c) -> p a c", a=2) for m in range(3))
        ec = sb("ec", [P, C, NF])
        shi = sb("shi", [P, C, 2], I32)
        sidx = sb("sidx", [P, C], I32)
        srow = sb("srow", [P, 2, U * P], I32)
        drow = sb("drow", [P, 2, U * P], I32)
        att = sb("att", [R, 2, U * P])
        npp = sb("npp", [P, 1])
        xb = sb("xb", [P, 2, JT, H])
        dist = xb[:].rearrange("p q j f -> p (q j f)")[:, 0:2 * U * P].rearrange("p (a e) -> p a e", a=2)
        mask = sb("mask", [P, 2, 2, U * P], F16)
        bc = sb("bc", [P, U, NF])
        bsh = sb("bsh", [P, U, 2], I32)
        gidx = sb("gidx", [P, 2, U], I32)
        scidx = sb("scidx", [P, 2, U], I32)
        xg = sb("xg", [P, 2, U, H + 1])
        zq = sb("zq", [P, U, 2])
        zi = sb("zi", [P, U, 2], I32)
        zi2 = sb("zi2", [P, U, 2], I32)
        zi3 = sb("zi3", [P, U, 2], I32)
        zfs = sb("zfs", [P, 2, U])
        zfd = sb("zfd", [P, U])
        oh = sb("oh", [P, U, NZ], BF16)
        ohT = sb("ohT", [NZ, U * P], BF16)
        hT = sb("hT", [H + 1, U * P])
        junk = sb("junk", [P, 2, JZ])
        junkd = sb("junkd", [P, 2, P])
        junka = sb("junka", [P, U, NZ])
        adap = sb("adap", [P, U])
        same = sb("same", [P, 2, U, P])
        dup = sb("dup", [P, U])
        dupn = sb("dupn", [P, U])
        cut = sb("cut", [P, 2, U])
        sx = sb("sx", [P, U])
        nm = sb("nm", [P, U])
        hn = sb("hn", [P, U, H])
        sq = sb("sq", [P, U, H])
        nmr = sb("nmr", [P, U])
        ss = sb("ss", [P, U])
        sd = sb("sd", [P, U])
        rs = sb("rs", [P, U])
        cw = sb("cw", [P, U])
        gg = sb("gg", [P, U, H])
        gw = sb("gw", [P, U, H])
        gx = sb("gx", [P, 2, U, H])
        msg = sb("msg", [P, U, MW])
        sm = sb("sm", [P, 2, U, MW])
        dinv = sb("dinv", [P, J])
        dx = sb("dx", [P, 2, JT, H + 1])
        da = sb("da", [P, 2, JT, MW])
        dh = sb("dh", [P, 2, JT, H])
        dc = sb("dc", [P, 2, JT, H])
        dq = sb("dq", [P, 2, JT, H])
        dy = sb("dy", [P, 2, JT, H])
        do = sb("do", [P, 2, JT, H])
        rsum = sb("rsum", [P, 2, JT])
        rsq = sb("rsq", [P, 2, JT])
        rroot = sb("rroot", [P, 2, JT])
        rinv = {m: sb(f"rinv_{m}", [P, 2, JT]) for m in "abc"}
        rtot = sb("rtot", [P, 2, JT])
        itot = sb("itot", [P, 2, JT])
        rdeg = sb("rdeg", [P, 2, JT])
        fac = sb("fac", [P, 2 * JT])
        fac2 = sb("fac2", [P, 2 * JT])
        ones = sb("ones", [P, 2 * JT])
        assert 6 * C <= 2 * JT * H and 2 * U * P <= 2 * JT * H

        p_z = ps("p_z", [P, 2, 512])
        p_h = ps("p_h", [H, 512])
        p_g = ps("p_g", [P, U, H])
        p_t = ps("p_t", [NZ, U * P], BF16)
        p_v = ps("p_v", [P, 8, P])
        p_s = ps("p_s", [P, U, MW])

        s_const = sem("s_const")
        s_cols = sem("s_cols")
        s_iota = sem("s_iota")
        s_spare = sem("s_spare")
        s_zero = sem("s_zero")
        s_cleared = [sem(f"s_cleared{q}") for q in range(2)]
        s_zeroed = [None] + [sem(f"s_zeroed{l}") for l in (1, 2)]
        s_u = sem("s_u")
        s_uc = sem("s_uc")
        s_sin = sem("s_sin")
        s_arg = sem("s_arg")
        s_set = sem("s_set")
        s_nop = {e: sem(f"s_nop_{e}") for e in ("pool", "act", "dve", "pe", "sp")}
        s_row = [sem(f"s_row{q}") for q in range(2)]
        s_att = [sem(f"s_att{q}") for q in range(2)]
        s_dist = sem("s_dist")
        s_mask = sem("s_mask")
        s_zp = sem("s_zp")
        s_zr = sem("s_zr")
        s_same = sem("s_same")
        s_chx = sem("s_chx")
        s_chy = sem("s_chy")
        s_oh = sem("s_oh")
        s_tr = sem("s_tr")
        s_trc = sem("s_trc")
        s_tv = sem("s_tv")
        s_ad = sem("s_ad")
        s_hid = sem("s_hid")
        s_silu = sem("s_silu")
        s_gate = sem("s_gate")
        s_gru = sem("s_gru")
        s_gidx = sem("s_gidx")
        s_gat = [sem(f"s_gat{q}") for q in range(2)]
        s_nm = sem("s_nm")
        s_ss = sem("s_ss")
        s_nmr = sem("s_nmr")
        s_hn = sem("s_hn")
        s_msg = sem("s_msg")
        s_sidx = sem("s_sidx")
        s_sum = sem("s_sum")
        s_smc = sem("s_smc")
        s_sca = [sem(f"s_sca{q}") for q in range(2)]
        L = []
        for l in (1, 2):
            L.append(dict(
                row=[sem(f"t{l}_row{q}") for q in range(2)], same=sem(f"t{l}_same"), gidx=sem(f"t{l}_gidx"),
                gat=[sem(f"t{l}_gat{q}") for q in range(2)], sum=sem(f"t{l}_sum"), smc=sem(f"t{l}_smc"),
                sidx=sem(f"t{l}_sidx"), stage=sem(f"t{l}_stage"), sca=[sem(f"t{l}_sca{q}") for q in range(2)]))
        d_x = [[sem(f"d{l}_x{q}") for q in range(2)] for l in range(3)]
        d_a = [[sem(f"d{l}_a{q}") for q in range(2)] for l in range(3)]
        d_acc = [[sem(f"d{l}_acc{q}") for q in range(2)] for l in range(3)]
        d_used = sem("d_used")
        d_made = [sem(f"d{l}_made") for l in range(3)]
        d_out = [[sem(f"d{l}_out{q}") for q in range(2)] for l in range(3)]
        d_ch = {m: sem(f"d_ch{m}") for m in ("a", "b", "c", 1, 2)}
        d_req = {m: sem(f"d_req{m}") for m in "abc"}
        d_ans = {m: sem(f"d_ans{m}") for m in "abc"}
        d_deg = sem("d_deg")
        d_tot = sem("d_tot")
        d_h = sem("d_h")
        d_n = sem("d_n")
        d_xb = sem("d_xb")
        d_st = sem("d_st")
        d_h2 = sem("d_h2")
        d_gm = sem("d_gm")
        d_y = sem("d_y")
        d_yout = sem("d_yout")

        block = ctx.enter_context(nc.Block())

        def hold(eng, name, s, v):
            eng.wait_ge(s, v)
            eng.nop().then_inc(s_nop[name], 1)

        def rows_of(table, n, t):
            w = n * table.shape[1]
            return table[0:NP, :].rearrange("(p j) f -> p (j f)", p=P)[:, bass.ds(t * w, w)]

        ZR = 56

        def zero_table(eng, table, earlier):
            view = table[0:NP, :].rearrange("(p j) f -> p (j f)", p=P)
            w = ZR * table.shape[1]
            for c in range(J // ZR):
                n = earlier + c
                if n >= 2:
                    eng.wait_ge(s_cleared[n % 2], 16 * (n // 2))
                eng.dma_start(view[:, c * w:(c + 1) * w], zero[:, 0:w]).then_inc(s_cleared[n % 2], 16)

        ZT = J // ZR
        ZS = J // (NB // 2)

        def zero_slice(eng, l, i):
            w = ZS * H
            eng.dma_start(sums[l][1][0:NP, :].rearrange("(p j) f -> p (j f)", p=P)[:, bass.ds(i * w, w)],
                          zero[:, 0:w]).then_inc(s_zeroed[l], 16)

        def pair_of(buf, w):
            return buf[:].rearrange("p q j f -> p (q j f)")[:, 0:2 * JT * w]

        @block.sync
        def _(sp):
            def dense_0():
                def load(i):
                    sp.dma_start(pair_of(dx, H + 1), rows_of(xm, 2 * JT, i)).then_inc(d_x[0][0], 16)
                    sp.dma_start(pair_of(da, MW), rows_of(sums[0][0], 2 * JT, i)).then_inc(d_a[0][0], 16)

                def store(i):
                    hold(sp, "sp", d_made[0], i + 1)
                    o = pair_of(do, H)
                    sp.dma_start(rows_of(gtab[0], 2 * JT, i), o).then_inc(d_out[0][0], 16)
                    sp.dma_start(rows_of(sums[1][0], 2 * JT, i), o).then_inc(d_out[0][0], 16)

                def store_x1(i):
                    hold(sp, "sp", d_y, i * 2 + 2)
                    sp.dma_start(rows_of(x1tab, 2 * JT, i), pair_of(dy, H)).then_inc(d_yout, 16)

                def turn(i):
                    hold(sp, "sp", d_used, i + 1)
                    hold(sp, "sp", d_deg, i * 2 + 2)
                    hold(sp, "sp", d_xb, i * 2 + 2)
                    hold(sp, "sp", d_st, i * 2 + 2)
                    load(i + 1)
                    if not isinstance(i, int):
                        store(i - 1)
                    store_x1(i)

                load(0)
                turn(0)
                with sp.Fori(1, PAIRS - 1) as i:
                    turn(i)
                store(PAIRS - 2)
                store_x1(PAIRS - 1)
                store(PAIRS - 1)
                sp.wait_ge(d_yout, 16 * PAIRS)
                sp.wait_ge(d_out[0][0], 32 * PAIRS)

            def dense_12(l):
                def load_sums(i, r):
                    q = r % 2
                    sp.dma_start(pair_of((da, dx)[q], H), rows_of(sums[l][0], 2 * JT, i * 2 + r)).then_inc(d_a[l][q], 16)

                def load_x1(i, r):
                    q = r % 2
                    if l == 2:
                        sp.dma_start(pair_of((dh, dc)[q], H), rows_of(x1tab, 2 * JT, i * 2 + r)).then_inc(d_x[l][q], 16)

                def store(i, r):
                    q = r % 2
                    hold(sp, "sp", d_made[l], i * 2 + r + 1)
                    o = pair_of((do, dy)[q], H)
                    for table in ((gtab[1], sums[2][0]) if l == 1 else (out,)):
                        sp.dma_start(rows_of(table, 2 * JT, i * 2 + r), o).then_inc(d_out[l][q], 16)

                def turn(i, r):
                    if l == 2:
                        hold(sp, "sp", d_ch[l], (i * 2 + r + 1) * CHAIN_D[l])
                        load_sums(i, r + 2)
                        store(i, r)
                        load_x1(i, r + 2)
                    else:
                        store(i, r)
                        load_sums(i, r + 2)

                for r in range(2):
                    load_sums(0, r)
                    load_x1(0, r)
                with sp.Fori(0, (PAIRS - 2) // 2) as i:
                    turn(i, 0)
                    turn(i, 1)
                for r in range(2):
                    store((PAIRS - 2) // 2, r)
                for q in range(2):
                    sp.wait_ge(d_out[l][q], 16 * STORES[l] * PAIRS // 2)

            sp.dma_start(dsti[:], dst_col).then_inc(s_cols, 16)
            sp.dma_start(srci[:], src_col).then_inc(s_cols, 16)
            sp.dma_start(wcol[:], w_col).then_inc(s_cols, 16)
            sp.dma_start(ztab_i[:], types).then_inc(s_cols, 16)
            def load_batch(i, r):
                q = r % 2
                b = i * 2 + r
                cols = bass.ds(b * (U * P), U * P)
                sp.dma_start(srow[:, q, :], src_row[0:1, cols].to_broadcast([P, U * P])).then_inc(s_row[q], 16)
                sp.dma_start(drow[:, q, :], dst_row[0:1, cols].to_broadcast([P, U * P])).then_inc(s_row[q], 16)

            def load_att(i, r):
                q = r % 2
                sp.dma_start(att[:, q, :], attrT[:, bass.ds((i * 2 + r) * (U * P), U * P)]).then_inc(s_att[q], 16)

            def prefetch(i, r):
                b = i * 2 + r
                hold(sp, "sp", s_same, b * U)
                load_batch(i, r + 1)
                hold(sp, "sp", s_hid, b * 2)
                load_att(i, r + 1)

            for r in range(2):
                load_batch(0, r)
                load_att(0, r)

            sp.wait_ge(s_zero, 1)
            zero_table(sp, sums[0][0], 0)
            prefetch(0, 1)
            zero_table(sp, sums[0][1], ZT)
            for q in range(2):
                sp.dma_start(sums[0][q][NP:NP + P, :], zero[:, 0:MW]).then_inc(s_cleared[q], 16)
            for l in (1, 2):
                for q in range(2):
                    sp.dma_start(sums[l][q][NP:NP + P, :], zero[:, 0:H]).then_inc(s_zeroed[l], 16)

            prefetch(0, 2)
            zero_slice(sp, 1, 0)
            with sp.Fori(1, (NB - 2) // 2) as i:
                prefetch(i, 1)
                prefetch(i, 2)
                zero_slice(sp, 1, i)
            zero_slice(sp, 1, (NB - 2) // 2)

            for l in range(3):
                if l > 0:
                    t = L[l - 1]

                    def load_rows(i, r, t=t):
                        q = r % 2
                        cols = bass.ds((i * 2 + r) * (U * P), U * P)
                        sp.dma_start(srow[:, q, :], src_row[0:1, cols].to_broadcast([P, U * P])).then_inc(t["row"][q], 16)

                    if l == 1:
                        sp.wait_ge(s_same, NB * U)
                    else:
                        sp.wait_ge(L[0]["same"], NB)
                    load_rows(0, 0)
                    load_rows(0, 1)
                    with sp.Fori(0, (NB - 2) // 2) as i:
                        for r in (1, 2):
                            hold(sp, "sp", t["same"], i * 2 + r)
                            load_rows(i, r + 1)
                        if l == 1:
                            zero_slice(sp, 2, i)
                    if l == 1:
                        zero_slice(sp, 2, (NB - 2) // 2)
                sca = s_sca if l == 0 else L[l - 1]["sca"]
                for q in range(2):
                    sp.wait_ge(sca[q], 16 * C // 2)

                if l == 0:
                    dense_0()
                else:
                    dense_12(l)

        @block.gpsimd
        def _(pool):
            pool.iota(iota_f[:], [[1, JZ]], base=0, channel_multiplier=0,
                      allow_small_or_imprecise_dtypes=True).then_inc(s_iota, 1)
            pool.iota(iota_b[:], [[1, NZ]], base=0, channel_multiplier=0,
                      allow_small_or_imprecise_dtypes=True).then_inc(s_iota, 1)
            pool.iota(part[:], [[0, 1]], base=0, channel_multiplier=1,
                      allow_small_or_imprecise_dtypes=True).then_inc(s_iota, 1)
            pool.iota(ncentre[:], [[0, 1]], base=-(JN - 1) // 2, channel_multiplier=-JN,
                      allow_small_or_imprecise_dtypes=True).then_inc(s_iota, 1)
            pool.memset(upto[:], 1.0).then_inc(s_iota, 1)
            pool.memset(ident[:], 0.0).then_inc(s_iota, 1)
            pool.wait_ge(s_iota, 6)
            pool.affine_select(out=upto[:], in_=upto[:], compare_op=ALU.is_ge, fill=0.0, base=0,
                               pattern=[[-1, P]], channel_multiplier=1).then_inc(s_iota, 1)
            pool.affine_select(out=ident[:], in_=ident[:], compare_op=ALU.not_equal, fill=1.0, base=0,
                               pattern=[[-1, P]], channel_multiplier=1).then_inc(s_iota, 1)

            def edge_pass(table, width, dst_tables, s_gi, s_g, rows, s_si, s_sm, s_sc, rows_free, zeroed):
                def gather(q, k):
                    pool.indirect_dma_start(rows[:, q, k, :], None, table,
                                            bass.IndirectOffsetOnAxis(gidx[:, q, k:k + 1], 0)).then_inc(s_g[q], 16)

                def scatter(i, r, k):
                    c = U * r + k
                    q = c % 2
                    before_it = i * U + c // 2
                    if isinstance(before_it, int):
                        if before_it > 0:
                            pool.wait_ge(s_sc[q], 16 * before_it)
                    else:
                        hold(pool, "pool", s_sc[q], before_it * 16)
                    pool.indirect_dma_start(dst_tables[q], bass.IndirectOffsetOnAxis(scidx[:, r % 2, k:k + 1], 0),
                                            sm[:, r % 2, k, 0:width], None, compute_op=ALU.add).then_inc(s_sc[q], 16)

                def ready(i, r):
                    b = i * 2 + r
                    hold(pool, "pool", s_gi, b + 1)
                    s_free, per = rows_free
                    if isinstance(b, int):
                        if b >= 2:
                            hold(pool, "pool", s_free, (b - 1) * per)
                    else:
                        hold(pool, "pool", s_free, (b - 1) * per)

                def sums_ready(i, r):
                    b = i * 2 + r
                    hold(pool, "pool", s_sm, b + 1)
                    hold(pool, "pool", s_si, b + 1)

                def step(i, r, first=False):
                    ready(i, r)
                    for k in range(U):
                        gather(r % 2, k)
                        if k == LAG:
                            sums_ready(i, r - 2)
                        if k >= LAG:
                            scatter(i, r - 2, k - LAG)
                        elif not first:
                            scatter(i, r - 3, U + k - LAG)

                for r in range(2):
                    ready(0, r)
                    for k in range(U):
                        gather(r, k)
                for s, v in zeroed:
                    pool.wait_ge(s, v)
                step(0, 2, first=True)
                step(0, 3)
                with pool.Fori(1, (NB - 2) // 2) as i:
                    step(i, 2)
                    step(i, 3)
                for k in range(LAG):
                    scatter((NB - 2) // 2, -1, U + k - LAG)
                for r in range(2):
                    sums_ready((NB - 2) // 2, r)
                    for k in range(U):
                        scatter((NB - 2) // 2, r, k)

            def accumulate(l):
                def step(i, r):
                    q = r % 2
                    hold(pool, "pool", d_a[l][q], (half(i, r) + 1) * 16)
                    for m in range(2):
                        pool.dma_start(pair_of((da, dx)[q], H)[:, m * JT * H:(m + 1) * JT * H],
                                       rows_of(sums[l][1], JT, i * 4 + (2 * r + m)),
                                       accum_op=ALU.add).then_inc(d_acc[l][q], 16)
                in_pairs(pool, PAIRS, step)

            def dense_0():
                def add_sums(i):
                    hold(pool, "pool", d_a[0][0], i * 16 + 16)
                    for m in range(2):
                        pool.dma_start(pair_of(da, MW)[:, m * JT * MW:(m + 1) * JT * MW],
                                       rows_of(sums[0][1], JT, i * 2 + m), accum_op=ALU.add).then_inc(d_acc[0][0], 16)

                def row_like(v):
                    return v.unsqueeze(1).to_broadcast([P, JT, H])

                def step(i, last=False):
                    for q in range(2):
                        pool.wait_ge(d_x[0][0], i * 16 + 16)
                        if not isinstance(i, int) or i > 0:
                            pool.wait_ge(d_y, i * 2)
                        pool.tensor_tensor(xb[:, q, :, :], dx[:, q, :, 0:H], row_like(bet[:]), ALU.add).then_inc(d_xb, 1)
                    for q in range(2):
                        pool.wait_ge(d_tot, i + 1)
                        if not isinstance(i, int) or i > 0:
                            pool.wait_ge(d_n, i * 2)
                        pool.tensor_tensor(st[:, q, :, :], da[:, q, :, 0:H],
                                           itot[:, q, :].unsqueeze(2).to_broadcast([P, JT, H]), ALU.mult).then_inc(d_st, 1)
                    for q in range(2):
                        pool.wait_ge(d_h, i * 2 + q + 1)
                        pool.wait_ge(d_st, i * 2 + q + 1)
                        pool.tensor_tensor(st[:, q, :, :], dh[:, q, :, :], st[:, q, :, :], ALU.add).then_inc(d_h2, 1)
                    if not last:
                        add_sums(i + 1)
                    for q in range(2):
                        pool.wait_ge(d_n, i * 2 + q + 1)
                        pool.tensor_tensor(dh[:, q, :, :], dh[:, q, :, :], row_like(gam[:]), ALU.mult).then_inc(d_gm, 1)
                    for q in range(2):
                        pool.wait_ge(d_gm, i * 2 + q + 1)
                        if not isinstance(i, int) or i > 0:
                            pool.wait_ge(d_yout, i * 16)
                            pool.wait_ge(d_made[0], i)
                        pool.tensor_tensor(dy[:, q, :, :], dh[:, q, :, :], xb[:, q, :, :], ALU.add).then_inc(d_y, 1)

                add_sums(0)
                step(0)
                with pool.Fori(1, PAIRS - 1) as i:
                    step(i)
                step(PAIRS - 1, last=True)

            edge_pass(xm, MW, sums[0], s_gidx, s_gat, xg, s_sidx, s_smc, s_sca, (s_msg, 1), [(s_cleared[q], 16 * (ZT + 1)) for q in range(2)])
            for q in range(2):
                pool.wait_ge(s_sca[q], 16 * C // 2)
            dense_0()
            for l in (1, 2):
                t = L[l - 1]
                if l == 1:
                    pool.wait_ge(d_out[0][0], 32 * PAIRS)
                else:
                    for q in range(2):
                        pool.wait_ge(d_out[1][q], 16 * STORES[1] * PAIRS // 2)
                edge_pass(gtab[l - 1], H, sums[l], t["gidx"], t["gat"], gx, t["sidx"], t["smc"], t["sca"],
                          (t["sum"], 1), [(s_zeroed[l], 16 * (NB // 2) + 32)])
                for q in range(2):
                    pool.wait_ge(t["sca"][q], 16 * C // 2)
                accumulate(l)

        @block.scalar
        def _(act):
            act.dma_start(w1T_s[:], w1T).then_inc(s_const, 16)
            act.dma_start(b1_s[:], b1).then_inc(s_const, 16)
            act.dma_start(w2_s[0:H, :], w2T).then_inc(s_const, 16)
            act.dma_start(w2_s[H:H + 1, :], b2).then_inc(s_const, 16)
            act.dma_start(embT_s[:], embT).then_inc(s_const, 16)
            act.dma_start(adT_s[:], adaptT).then_inc(s_const, 16)
            act.dma_start(gam[:], gamma.to_broadcast([P, H])).then_inc(s_const, 16)
            act.dma_start(bet[:], beta.to_broadcast([P, H])).then_inc(s_const, 16)
            act.wait_ge(s_iota, 8)
            act.activation(identf[:], ident[:], ACT.Copy).then_inc(s_uc, 1)
            act.wait_ge(s_u, 1)
            act.activation(u_s[:], p_v[0:G, 0, 0:NZ], ACT.Copy).then_inc(s_uc, 1)
            act.wait_ge(s_u, 2)
            act.activation(tt_s[:], p_v[0:NZ, 1, 0:NZ], ACT.Copy).then_inc(s_uc, 1)
            act.wait_ge(s_arg, 1)
            act.activation(t1[:, 1, :], t1[:, 0, :], ACT.Sin, scale=PI / (2 * CUTOFF)).then_inc(s_sin, 1)

            def distances(i, r):
                q = r % 2
                b = i * 2 + r
                act.wait_ge(s_row[q], (half(i, r) + 1) * 32)
                if not isinstance(b, int) or b > 0:
                    act.wait_ge(s_mask, b * 2)
                for w, rows in enumerate((srow, drow)):
                    act.activation(dist[:, w, :], rows[:, q, :], ACT.Abs, bias=ncentre[:, 0:1]).then_inc(s_dist, 1)

            def hidden(i, r, m):
                b = i * 2 + r
                act.wait_ge(s_hid, b * 2 + m + 1)
                if m == 0 and (not isinstance(b, int) or b > 0):
                    act.wait_ge(s_gate, b)
                act.activation(hT[0:H, m * (U * P // 2):(m + 1) * (U * P // 2)], p_h[:, 0:U * P // 2],
                               ACT.Silu, bias=b1_s[:, 0:1]).then_inc(s_silu, 1)

            def copy_types(i, r):
                b = i * 2 + r
                act.wait_ge(s_tr, b + 1)
                if not (isinstance(b, int) and b == 0):
                    act.wait_ge(s_tv, b * 2)
                act.activation(ohT[:], p_t[:], ACT.Copy).then_inc(s_trc, 1)

            def messages(i, r):
                q = r % 2
                b = i * 2 + r
                first = isinstance(b, int) and b == 0
                act.wait_ge(s_nm, b + 1)
                for k in range(U):
                    last = act.activation(sq[:, k, :], xg[:, q, k, 0:H], ACT.Square, bias=nm[:, k:k + 1],
                                          accum_out=ss[:, k:k + 1])
                last.then_inc(s_ss, 1)
                act.wait_ge(s_ss, b * 2 + 1)
                act.activation(sd[:], ss[:], ACT.Sqrt, scale=1.0 / H, bias=epsc[:, 0:1]).then_inc(s_ss, 1)
                if not (isinstance(b, int) and b >= NB - 2):
                    distances(i, r + 2)
                act.wait_ge(s_nmr, b + 1)
                if not first:
                    act.wait_ge(s_msg, b)
                for k in range(U):
                    last = act.activation(hn[:, k, :], xg[:, q, k, 0:H], ACT.Relu, bias=nmr[:, k:k + 1],
                                          scale=rs[:, k:k + 1])
                last.then_inc(s_hn, 1)
                if not (isinstance(b, int) and b == NB - 1):
                    for m in range(2):
                        hidden(i, r + 1, m)
                    copy_types(i, r + 1)
                copy_sums(i, r, s_sum, s_smc, s_sca, MW)

            def copy_sums(i, r, s_sum, s_smc, s_sca, w):
                b = i * 2 + r
                act.wait_ge(s_sum, b + 1)
                if not isinstance(b, int) or b >= 2:
                    landed(act, i, r, s_sca)
                act.activation(sm[:, r % 2, :, 0:w], p_s[:, :, 0:w], ACT.Copy).then_inc(s_smc, 1)

            act.wait_ge(s_iota, 8)
            act.wait_ge(s_const, 8 * 16)
            act.wait_ge(s_set, SETUP)
            distances(0, 0)
            distances(0, 1)
            for m in range(2):
                hidden(0, 0, m)
            copy_types(0, 0)
            in_pairs(act, NB, messages, last_two=True)

            def norm(m, i):
                for q in range(2):
                    act.wait_ge(d_req[m], i * 4 + q + 1)
                    act.activation(dq[:, q, :, :], dc[:, q, :, :], ACT.Square).then_inc(d_ans[m], 1)
                for q in range(2):
                    act.wait_ge(d_req[m], i * 4 + q + 3)
                    act.activation(rroot[:, q, :], rsq[:, q, :], ACT.Sqrt, scale=1.0 / H, bias=epsc[:, 0:1]).then_inc(d_ans[m], 1)

            def dense_step(i):
                norm("a", i)
                act.wait_ge(d_acc[0][0], i * 32 + 32)
                if not isinstance(i, int) or i > 0:
                    act.wait_ge(d_used, i)
                for q in range(2):
                    act.activation(rdeg[:, q, :], da[:, q, :, H + 1], ACT.Sqrt, bias=1.0).then_inc(d_deg, 1)
                if not isinstance(i, int) or i > 0:
                    norm("c", i - 1)
                norm("b", i)

            dense_step(0)
            with act.Fori(1, PAIRS) as i:
                dense_step(i)
            norm("c", PAIRS - 1)
            for l in (1, 2):
                t = L[l - 1]
                in_pairs(act, NB, lambda i, r: copy_sums(i, r, t["sum"], t["smc"], t["sca"], H))

        @block.tensor
        def _(pe):
            pe.wait_ge(s_const, 8 * 16)
            pe.matmul(p_v[0:G, 0, 0:NZ], adT_s[:], embT_s[:], start=True, stop=True).then_inc(s_u, 1)
            pe.wait_ge(s_uc, 2)
            pe.matmul(p_v[0:NZ, 1, 0:NZ], u_s[:], embT_s[:], start=True, stop=True).then_inc(s_u, 1)
            pe.wait_ge(s_uc, 3)
            pe.wait_ge(s_set, SETUP)

            def lookups(i, r, ks):
                b = i * 2 + r
                first = isinstance(b, int) and b == 0
                if 0 in ks:
                    pe.wait_ge(s_mask, b * 2 + 2)
                for k in ks:
                    for w in range(2):
                        if not (first and k == 0):
                            pe.wait_ge(s_zr, b * (2 * U) + 2 * k + w - 1)
                        for m in range(2):
                            last = pe.matmul(p_z[:, w, 0:JZ], mask[:, r % 2, w, k * P:(k + 1) * P], ztab[:, m, :],
                                             start=(m == 0), stop=(m == 1))
                        last.then_inc(s_zp, 1)

            def hidden(i, r, m):
                b = i * 2 + r
                hw = U * P // 2
                if m == 0:
                    hold(pe, "pe", s_att[r % 2], (half(i, r) + 1) * 16)
                if not (isinstance(b, int) and b == 0 and m == 0):
                    hold(pe, "pe", s_silu, b * 2 + m)
                pe.matmul(p_h[:, 0:hw], w1T_s[:], att[:, r % 2, m * hw:(m + 1) * hw], start=True, stop=True).then_inc(s_hid, 1)

            def transposes(i, r):
                b = i * 2 + r
                pe.wait_ge(s_oh, b + 1)
                if not (isinstance(b, int) and b == 0):
                    pe.wait_ge(s_trc, b)
                for k in range(U):
                    last = pe.transpose(p_t[:, k * P:(k + 1) * P], oh[:, k, :], ident[:])
                last.then_inc(s_tr, 1)

            def step(i, r, ahead=True, further=True):
                b = i * 2 + r
                first = isinstance(b, int) and b == 0
                def look(*ks):
                    if ahead:
                        lookups(i, r + 1, ks)

                def gates(*ks):
                    if ks[0] == 0:
                        pe.wait_ge(s_silu, b * 2 + 2)
                        if not first:
                            pe.wait_ge(s_gru, b)
                    for k in ks:
                        last = pe.matmul(p_g[:, k, :], hT[:, k * P:(k + 1) * P], w2_s[:], start=True, stop=True)
                    if ks[-1] == U - 1:
                        last.then_inc(s_gate, 1)

                look(1)
                pe.wait_ge(s_trc, b + 1)
                for g, ks in enumerate(GROUPS):
                    if not first:
                        pe.wait_ge(s_ad, (b - 1) * U + ks[-1] + 1)
                    for k in ks:
                        for m in range(3):
                            last = pe.matmul(p_v[:, k, 0:NZ], ohT[:, k * P:(k + 1) * P], tt_b[:, m, :],
                                             start=(m == 0), stop=(m == 2))
                        if k == ks[-1]:
                            last.then_inc(s_tv, 1)
                        if k in (1, 3):
                            look(2 + k // 2)
                look(4)
                gates(0, 1)
                if ahead:
                    hidden(i, r + 1, 0)
                look(5)
                gates(2, 3, 4)
                look(6)
                gates(5, 6)
                if ahead:
                    hidden(i, r + 1, 1)
                if further:
                    lookups(i, r + 2, (0,))
                sum_batch(i, r, msg, MW, s_msg, s_sum, s_smc, (lambda: transposes(i, r + 1)) if ahead else None)

            def sum_batch(i, r, rows, w, s_rows, s_sum, s_smc, between=None):
                b = i * 2 + r
                first = isinstance(b, int) and b == 0
                pe.wait_ge(s_rows, b + 1)
                if not first:
                    pe.wait_ge(s_smc, b)
                for k in range(U):
                    if k == U // 2 + 1 and between:
                        between()
                    last = pe.matmul(p_s[:, k, 0:w], same[:, r % 2, k, :], rows[:, k, :], start=True, stop=True)
                last.then_inc(s_sum, 1)

            for m in range(2):
                hidden(0, 0, m)
            lookups(0, 0, range(U))
            lookups(0, 1, (0,))
            transposes(0, 0)

            def step_or_last(i, r):
                b = i * 2 + r
                left = NB - 1 - b if isinstance(b, int) else 2
                step(i, r, ahead=left >= 1, further=left >= 2)

            in_pairs(pe, NB, step_or_last, last_two=True)

            for l in (1, 2):
                t = L[l - 1]

                def step(i, r):
                    q = r % 2
                    pe.wait_ge(t["gat"][q], (half(i, r) + 1) * (16 * U))
                    sum_batch(i, r, gx[:, q, :, :], H, t["same"], t["sum"], t["smc"])
                in_pairs(pe, NB, step)

        @block.vector
        def _(dve):
            dve.memset(zero[:], 0.0).then_inc(s_zero, 1)
            n = [0]

            def do_(ins):
                n[0] += 1
                ins.then_inc(s_set, 1)
                dve.wait_ge(s_set, n[0])

            do_(dve.memset(hT[:], 1.0))
            do_(dve.memset(msg[:], 1.0))
            do_(dve.memset(epsc[:], EPS))
            do_(dve.memset(ones[:], 1.0))
            dve.wait_ge(s_iota, 8)
            dve.wait_ge(s_cols, 64)
            dve.wait_ge(s_uc, 3)
            rest = tt_s[:]
            for m in range(3):
                do_(dve.tensor_copy(tt_b[:, m, :], rest))
                if m < 2:
                    do_(dve.tensor_tensor(tt_r[:, m, :], rest, tt_b[:, m, :], ALU.subtract))
                    rest = tt_r[:, m, :]
            do_(dve.tensor_scalar(t0[:, 0, :], wcol[:], 1.0 / (2 * CUTOFF), ROUND, ALU.mult, ALU.add))
            do_(dve.tensor_scalar(t0[:, 1, :], t0[:, 0, :], -ROUND, None, ALU.add))
            n[0] += 1
            dve.scalar_tensor_tensor(t1[:, 0, :], t0[:, 1, :], -2.0 * CUTOFF, wcol[:], ALU.mult, ALU.add).then_inc(s_arg, 1)
            n[0] -= 1
            for m in range(1, NPACK):
                do_(dve.scalar_tensor_tensor(ztab_i[:, 0:JZ], ztab_i[:, m * JZ:(m + 1) * JZ], float(128 ** m),
                                             ztab_i[:, 0:JZ], ALU.mult, ALU.add))
            do_(dve.tensor_scalar(ztab_i[:, JZ:2 * JZ], ztab_i[:, 0:JZ], LOW, None, ALU.logical_shift_right))
            do_(dve.tensor_scalar(ztab_i[:, 2 * JZ:3 * JZ], ztab_i[:, 0:JZ], 2 ** LOW - 1, None, ALU.bitwise_and))
            do_(dve.tensor_copy(ztab[:, 0, :], ztab_i[:, JZ:2 * JZ]))
            do_(dve.tensor_scalar(ztab[:, 1, :], ztab_i[:, 2 * JZ:3 * JZ], 2.0 ** -LOW, None, ALU.mult))
            do_(dve.tensor_copy(srcf[:], srci[:]))
            do_(dve.tensor_copy(ec[:, :, ESRC], srcf[:]))
            do_(dve.tensor_scalar(npp[:, 0:1], part[:], float(NP), None, ALU.add))
            do_(dve.tensor_scalar(ec[:, :, SPARE], srcf[:], -1.0, npp[:, 0:1], ALU.mult, ALU.add))
            do_(dve.tensor_tensor(ec[:, :, BASE], srcf[:], ec[:, :, SPARE], ALU.subtract))
            dve.wait_ge(s_sin, 1)
            do_(dve.tensor_tensor(t0[:, 0, :], t1[:, 1, :], t1[:, 1, :], ALU.mult))
            do_(dve.tensor_scalar(t0[:, 1, :], t0[:, 0, :], -1.0, 1.0, ALU.mult, ALU.add))
            do_(dve.scalar_tensor_tensor(ec[:, :, CUT], wcol[:], CUTOFF, t0[:, 1, :], ALU.is_lt, ALU.mult))
            for w, idx in enumerate((srci[:], dsti[:, 0:C])):
                do_(dve.tensor_scalar(t0[:, 0, :], idx, 0.5, 1.0 / JN, ALU.add, ALU.mult))
                do_(dve.tensor_scalar(t0[:, 1, :], t0[:, 0, :], -0.5, ROUND, ALU.add, ALU.add))
                do_(dve.tensor_scalar(t0[:, 0, :], t0[:, 1, :], -ROUND, None, ALU.add))
                do_(dve.scalar_tensor_tensor(t1[:, 0, :], t0[:, 0, :], -float(JN), idx, ALU.mult, ALU.add))
                do_(dve.tensor_scalar(t2[:, 0, :], t1[:, 0, :], float(JZ), None, ALU.is_ge))
                do_(dve.scalar_tensor_tensor(t2[:, 1, :], t1[:, 0, :], float(2 * JZ), t2[:, 0, :], ALU.is_ge, ALU.add))
                do_(dve.scalar_tensor_tensor(ec[:, :, CSRC + w], t2[:, 1, :], -float(JZ), t1[:, 0, :], ALU.mult, ALU.add))
                do_(dve.tensor_scalar(shi[:, :, w], t2[:, 1, :], 7.0, None, ALU.mult))
            for r in range(2):
                dve.tensor_copy(gidx[:, r, :], dsti[:, r * U:(r + 1) * U]).then_inc(s_gidx, 1)
            assert n[0] == SETUP, n[0]

            class Steps:

                def __init__(self, s, base):
                    self.s, self.base, self.n = s, base, 0

                def __call__(self, ins):
                    self.n += 1
                    ins.then_inc(self.s, 1)

                def done(self, k=None):
                    dve.wait_ge(self.s, self.base + (self.n if k is None else k))

            def masks(i, r, w):
                b = i * 2 + r
                dve.wait_ge(s_dist, b * 2 + w + 1)
                if not isinstance(b, int) or b >= 2:
                    dve.wait_ge(s_zp, (b - 1) * (2 * U))
                dve.tensor_scalar(mask[:, r % 2, w, :], dist[:, w, :], JN / 2, None, ALU.is_lt).then_inc(s_mask, 1)

            def step(i, r, types=True, messages=True):
                q = r % 2
                b = i * 2 + r
                first = isinstance(b, int) and b == 0
                c = b - 1
                q1 = (r - 1) % 2
                cx = Steps(s_chx, b * CHAIN_X)
                cy = Steps(s_chy, c * CHAIN_Y)
                cols = bass.ds(b * U, U)
                if messages:
                    hold(dve, "dve", s_gat[q1], (half(i, r - 1) + 1) * (16 * U))
                    cy(dve.reduce_sum(sx[:], xg[:, q1, :, 0:H], axis=AX))
                if types:
                    if not first:
                        cx.done(0)
                    cx(dve.tensor_copy(bc[:], ec[:, cols, :]))
                    cx(dve.tensor_copy(bsh[:], shi[:, cols, :]))
                if messages:
                    cy.done()
                    dve.tensor_scalar(nm[:], sx[:], -1.0 / H, None, ALU.mult).then_inc(s_nm, 1)
                    if not (isinstance(b, int) and b == NB):
                        dve.tensor_copy(gidx[:, q1, :], dsti[:, bass.ds(b * U + U, U)]).then_inc(s_gidx, 1)

                def logit(k):
                    if k in (GROUPS[0][0], GROUPS[1][0]):
                        dve.wait_ge(s_tv, c * 2 + (1 if k == 0 else 2))
                    dve.scalar_tensor_tensor(junka[:, k, :], iota_f[:, 0:NZ], zfs[:, q1, k:k + 1], p_v[:, k, 0:NZ],
                                             ALU.is_equal, ALU.mult, accum_out=adap[:, k:k + 1]).then_inc(s_ad, 1)

                def factors():
                    dve.wait_ge(s_ss, c * 2 + 2)
                    cy(dve.reciprocal(rs[:], sd[:]))
                    cy(dve.tensor_tensor(cw[:], cut[:, q1, :], xg[:, q1, :, H], ALU.mult))
                    if not isinstance(b, int) or b >= 3:
                        landed(dve, i, r - 1, s_sca)
                        hold(dve, "dve", s_sidx, c)
                    dve.tensor_copy(scidx[:, q1, :], sidx[:, bass.ds(c * U, U)]).then_inc(s_sidx, 1)
                    cy.done(cy.n - 1)
                    dve.tensor_tensor(nmr[:], nm[:], rs[:], ALU.mult).then_inc(s_nmr, 1)

                if types:
                    dve.wait_ge(s_row[q], (half(i, r) + 1) * 32)
                    cx.done()
                for k in range(U):
                    for w in range(2):
                        if types:
                            dve.wait_ge(s_zp, b * (2 * U) + 2 * k + w + 1)
                            dve.scalar_tensor_tensor(junk[:, w, :], iota_f[:], bc[:, k, w:w + 1], p_z[:, w, 0:JZ],
                                                     ALU.is_equal, ALU.mult, accum_out=zq[:, k, w:w + 1]).then_inc(s_zr, 1)
                        if messages and w == 0 and k >= 3:
                            logit(k - 3)
                        if types and w == 1:
                            if k == 0 and (not isinstance(b, int) or b >= 2):
                                dve.wait_ge(s_sum, b - 1)
                            dve.scalar_tensor_tensor(same[:, q, k, :], srow[:, q, k * P:(k + 1) * P],
                                                     bc[:, k, ESRC:ESRC + 1], upto[:], ALU.is_equal, ALU.mult,
                                                     accum_out=dup[:, k:k + 1]).then_inc(s_same, 1)
                    if messages and k == 4:
                        factors()
                    if types and k >= 5 and not (isinstance(b, int) and b == NB - 1):
                        masks(i, r + 1, k - 5)
                if messages:
                    logit(U - 3)
                if types:
                    dve.wait_ge(s_zr, (b + 1) * (2 * U))
                    cx(dve.tensor_scalar(zi[:], zq[:], 2.0 ** LOW, None, ALU.mult))
                if messages:
                    logit(U - 2)
                if types:
                    cx.done()
                    cx(dve.tensor_tensor(zi2[:], zi[:], bsh[:], ALU.logical_shift_right))
                if messages:
                    logit(U - 1)
                if types:
                    cx.done()
                    cx(dve.tensor_scalar(zi3[:], zi2[:], 127, None, ALU.bitwise_and))
                if messages:
                    dve.wait_ge(s_ad, c * U + U)
                    dve.wait_ge(s_gate, c + 1)
                    dve.tensor_tensor(gg[:], p_g[:], adap[:].unsqueeze(2).to_broadcast([P, U, H]), ALU.add).then_inc(s_gru, 1)
                if types:
                    cx.done()
                    dve.tensor_copy(zfs[:, q, :], zi3[:, :, 0])
                    cx(dve.tensor_copy(zfd[:], zi3[:, :, 1]))
                if messages:
                    if not (isinstance(c, int) and c == 0):
                        dve.wait_ge(s_sum, c)
                    cy(dve.tensor_copy(msg[:, :, H], xg[:, q1, :, H]))
                    dve.wait_ge(s_gru, c + 1)
                    cy(dve.tensor_tensor(gw[:], gg[:], cw[:].unsqueeze(2).to_broadcast([P, U, H]), ALU.mult))
                if types:
                    dve.tensor_copy(cut[:, q, :], bc[:, :, CUT])
                    dve.wait_ge(s_same, (b + 1) * U)
                    cx(dve.scalar_tensor_tensor(dupn[:], dup[:], 2.0, bc[:, :, SPARE], ALU.min, ALU.mult))
                if messages:
                    cy.done()
                    dve.wait_ge(s_hn, c + 1)
                    dve.tensor_tensor(msg[:, :, 0:H], hn[:], gw[:], ALU.mult).then_inc(s_msg, 1)
                    assert cy.n == CHAIN_Y, cy.n
                if types:
                    cx.done()
                    if not first:
                        dve.wait_ge(s_tr, b)
                    for k in range(U):
                        last = dve.tensor_scalar(oh[:, k, :], iota_b[:], zfd[:, k:k + 1], None, ALU.is_equal)
                    last.then_inc(s_oh, 1)
                    cx(dve.tensor_tensor(sidx[:, cols], dupn[:], bc[:, :, BASE], ALU.add))
                    assert cx.n == CHAIN_X, cx.n

            for w in range(2):
                masks(0, 0, w)
            step(0, 0, messages=False)
            for r in (1, 2):
                step(0, r)
            with dve.Fori(1, (NB - 1) // 2) as i:
                step(i, 1)
                step(i, 2)
            step((NB - 1) // 2, 1)
            step((NB - 1) // 2, 2, types=False)

            def wide(v):
                return v.unsqueeze(2).to_broadcast([P, JT, H])

            def deviation(m, i, rows, step):
                first = step.n
                for q in range(2):
                    step(dve.reduce_sum(rsum[:, q, :], rows(q), axis=AX))
                for q in range(2):
                    step.done(first + q + 1)
                    dve.scalar_tensor_tensor(dc[:, q, :, :], wide(rsum[:, q, :]), -1.0 / H, rows(q), ALU.mult,
                                             ALU.add).then_inc(d_req[m], 1)
                for q in range(2):
                    dve.wait_ge(d_ans[m], i * 4 + q + 1)
                    dve.reduce_sum(rsq[:, q, :], dq[:, q, :, :], axis=AX).then_inc(d_req[m], 1)

            def inverse(m, i, step):
                for q in range(2):
                    dve.wait_ge(d_ans[m], i * 4 + q + 3)
                    step(dve.reciprocal(rinv[m][:, q, :], rroot[:, q, :]))

            def stage_a(i):
                later = not isinstance(i, int) or i > 0
                step = Steps(d_ch["a"], i * CHAIN_D["a"])
                dve.wait_ge(d_x[0][0], i * 16 + 16)
                deviation("a", i, lambda q: dx[:, q, :, 0:H], step)
                dve.wait_ge(d_acc[0][0], i * 32 + 32)
                step(dve.tensor_scalar(rtot[:], da[:, :, :, H], 1e-8, None, ALU.max))
                step.done()
                if later:
                    dve.wait_ge(d_st, i * 2)
                dve.reciprocal(itot[:], rtot[:]).then_inc(d_tot, 1)
                inverse("a", i, step)
                if later:
                    dve.wait_ge(d_y, i * 2)
                for q in range(2):
                    step.done(step.n - 1 + q)
                    dve.scalar_tensor_tensor(dh[:, q, :, :], dc[:, q, :, :], 0.0, wide(rinv["a"][:, q, :]), ALU.max,
                                             ALU.mult).then_inc(d_h, 1)
                dve.wait_ge(d_deg, i * 2 + 2)
                step(dve.reciprocal(dinv[:, bass.ds(i * (2 * JT), 2 * JT)], rdeg[:].rearrange("p q j -> p (q j)")))
                step.done()
                dve.nop().then_inc(d_used, 1)
                assert step.n == CHAIN_D["a"], step.n

            def stage_b(i):
                step = Steps(d_ch["b"], i * CHAIN_D["b"])
                dve.wait_ge(d_h2, i * 2 + 2)
                deviation("b", i, lambda q: st[:, q, :, :], step)
                inverse("b", i, step)
                for q in range(2):
                    step.done(step.n - 1 + q)
                    dve.tensor_tensor(dh[:, q, :, :], dc[:, q, :, :], wide(rinv["b"][:, q, :]), ALU.mult).then_inc(d_n, 1)
                assert step.n == CHAIN_D["b"], step.n

            def stage_c(i):
                step = Steps(d_ch["c"], i * CHAIN_D["c"])
                dve.wait_ge(d_y, i * 2 + 2)
                if not isinstance(i, int) or i > 0:
                    dve.wait_ge(d_out[0][0], i * 32)
                deviation("c", i, lambda q: dy[:, q, :, :], step)
                inverse("c", i, step)
                step.done()
                step(dve.tensor_tensor(fac[:], rinv["c"][:].rearrange("p q j -> p (q j)"),
                                       dinv[:, bass.ds(i * (2 * JT), 2 * JT)], ALU.mult))
                step.done()
                for q in range(2):
                    last = dve.scalar_tensor_tensor(do[:, q, :, :], dc[:, q, :, :], 0.0,
                                                    wide(fac[:, q * JT:(q + 1) * JT]), ALU.max, ALU.mult)
                last.then_inc(d_made[0], 1)
                assert step.n == CHAIN_D["c"], step.n

            stage_a(0)
            stage_b(0)
            with dve.Fori(1, PAIRS) as i:
                stage_a(i)
                stage_c(i - 1)
                stage_b(i)
            stage_c(PAIRS - 1)

            def dense(l):
                def rows(buf):
                    return pair_of(buf, H).rearrange("p (j f) -> p j f", f=H)

                def wide2(v):
                    return v.unsqueeze(2).to_broadcast([P, 2 * JT, H])

                def pair(i, r):
                    q = r % 2
                    b = i * 2 + r
                    step = Steps(d_ch[l], b * CHAIN_D[l])
                    if not isinstance(b, int) or b > 0:
                        dve.wait_ge(d_made[l], b)
                    step(dve.tensor_tensor(fac[:], dinv[:, bass.ds(b * (2 * JT), 2 * JT)], ones[:], ALU.mult))
                    step.done()
                    if l == 1:
                        step(dve.tensor_tensor(fac2[:], fac[:], fac[:], ALU.mult))
                    dve.wait_ge(d_acc[l][q], (half(i, r) + 1) * 32)
                    if not isinstance(b, int) or b >= 2:
                        dve.wait_ge(d_out[l][q], half(i, r) * (16 * STORES[l]))
                    if l == 1:
                        step.done()
                        dve.tensor_tensor(rows((do, dy)[q]), rows((da, dx)[q]), wide2(fac2[:]), ALU.mult).then_inc(d_made[l], 1)
                    else:
                        step(dve.tensor_tensor(rows((dq, st)[q]), rows((da, dx)[q]), wide2(fac[:]), ALU.mult))
                        step.done()
                        dve.wait_ge(d_x[l][q], (half(i, r) + 1) * 16)
                        dve.tensor_tensor(rows((do, dy)[q]), rows((dq, st)[q]), rows((dh, dc)[q]), ALU.add).then_inc(d_made[l], 1)
                    assert step.n == CHAIN_D[l], step.n
                in_pairs(dve, PAIRS, pair)

            for l in (1, 2):
                t = L[l - 1]
                for r in range(2):
                    dve.tensor_copy(gidx[:, r, :], dsti[:, r * U:(r + 1) * U]).then_inc(t["gidx"], 1)

                def step(i, r):
                    q = r % 2
                    b = i * 2 + r
                    cols = bass.ds(b * U, U)
                    if not isinstance(b, int) or b > 0:
                        hold(dve, "dve", t["same"], b)
                    dve.tensor_copy(bc[:, :, 0], srcf[:, cols]).then_inc(t["stage"], 1)
                    dve.wait_ge(t["stage"], b + 1)
                    dve.wait_ge(t["row"][q], (half(i, r) + 1) * 16)
                    if not isinstance(b, int) or b >= 2:
                        dve.wait_ge(t["sum"], b - 1)
                    for k in range(U):
                        last = dve.tensor_scalar(same[:, q, k, :], srow[:, q, k * P:(k + 1) * P], bc[:, k, 0:1], None, ALU.is_equal)
                    last.then_inc(t["same"], 1)
                    if not isinstance(b, int) or b >= 2:
                        landed(dve, i, r, t["sca"])
                        hold(dve, "dve", t["sidx"], b)
                    dve.tensor_copy(scidx[:, q, :], sidx[:, cols]).then_inc(t["sidx"], 1)
                    if not (isinstance(b, int) and b == NB - 1):
                        hold(dve, "dve", t["gat"][q], (half(i, r) + 1) * (16 * U))
                        dve.tensor_copy(gidx[:, q, :], dsti[:, bass.ds(b * U + 2 * U, U)]).then_inc(t["gidx"], 1)
                in_pairs(dve, NB, step)
                dense(l)


def kernel(x, src, dst, edge_attr_40, edge_weight, node_type_119, node_vec, L0_gnn_W1, L0_gnn_b1, L0_gnn_W2,
           L0_gnn_b2, L0_gnn_emb, L0_gnn_adaptW, L0_gnn_gamma, L0_gnn_beta):
    import numpy as np
    import concourse.bacc as bacc
    from concourse.bass_utils import run_bass_kernel_spmd

    def padded(a, n, fill=0):
        a = np.asarray(a)
        out = np.zeros((n,) + a.shape[1:], a.dtype)
        out[:a.shape[0]] = a
        if not isinstance(fill, int):
            out[a.shape[0]:] = fill
        return out

    spare = (NP + np.arange(E) % P).astype(np.int32)[np.asarray(src).shape[0]:]
    srcp = padded(src, E, spare)
    dstp = padded(dst, E)

    def by_chunk(a):
        return np.ascontiguousarray(a.reshape(C, P).T)

    arrays = {
        "xm": padded(np.concatenate([np.asarray(x), np.asarray(node_vec)[:, None]], axis=1), NP),
        "src_col": by_chunk(srcp),
        "dst_col": np.concatenate([by_chunk(dstp), np.zeros((P, 2 * U), dstp.dtype)], axis=1),
        "w_col": by_chunk(padded(edge_weight, E)),
        "src_row": srcp[None, :],
        "dst_row": dstp[None, :],
        "attrT": np.ascontiguousarray(padded(edge_attr_40, E).T),
        "types": padded(node_type_119, P * JN).reshape(P, JN),
        "w1T": np.ascontiguousarray(np.asarray(L0_gnn_W1).T),
        "b1": np.asarray(L0_gnn_b1)[:, None],
        "w2T": np.ascontiguousarray(np.asarray(L0_gnn_W2).T),
        "b2": np.asarray(L0_gnn_b2)[None, :],
        "embT": np.ascontiguousarray(np.asarray(L0_gnn_emb).T),
        "adaptT": np.ascontiguousarray(np.asarray(L0_gnn_adaptW).T),
        "gamma": np.asarray(L0_gnn_gamma)[None, :],
        "beta": np.asarray(L0_gnn_beta)[None, :],
    }
    nc = bacc.Bacc("TRN2", target_bir_lowering=False, num_devices=1)
    args = [nc.dram_tensor(k, a.shape, mybir.dt.from_np(a.dtype), kind="ExternalInput").ap() for k, a in arrays.items()]
    args.append(nc.dram_tensor("result", (NP, H), F32, kind="ExternalOutput").ap())
    build(nc, *args)
    got = run_bass_kernel_spmd(nc, [arrays], core_ids=[0])
    return got.results[0]["result"][:N]
```
